# Optimizing a Trainium2 kernel written in Bass

```python
import numpy as np
import jax
import jax.numpy as jnp

def _softmax(x, axis=-1):
    return jax.nn.softmax(x, axis=axis)

def _gelu(x):
    return jax.nn.gelu(x, approximate=True)

def _silu(x):
    return jax.nn.silu(x)

def _sigmoid(x):
    return jax.nn.sigmoid(x)

def _layernorm(x, axis=-1, eps=1e-05):
    m = jnp.mean(x, axis=axis, keepdims=True)
    v = jnp.var(x, axis=axis, keepdims=True)
    return (x - m) / jnp.sqrt(v + eps)

def _scatter_add(tgt, idx, src, axis=0):
    return tgt.at[idx].add(src)

def _segment_sum(src, seg, n):
    return jax.ops.segment_sum(src, seg, n)
kernel_name = 'mk_rec_standalone_d1_rec_r8_3b5bcd'

def setup_inputs(seed: int=0):
    np.random.seed(seed)
    _w = jnp.asarray

    def _rec_inputs():
        import jax
        import jax.numpy as jnp
        _rk = jax.random.key(seed)
        r_user_indices = jax.random.randint(jax.random.fold_in(_rk, 1), (2048,), 0, 1000, jnp.int32)
        return r_user_indices
    r_user_indices = _rec_inputs()

    def _L0_rec_setup():
        import jax, jax.numpy as jnp
        import numpy as np
        U, I, D, L, NNZ = (1000, 2000, 64, 2, 96000)
        N = U + I
        key = jax.random.key(seed)
        ks = jax.random.split(key, 10)
        return {'user_indices': jnp.arange(U, dtype=jnp.int64) if jax.config.jax_enable_x64 else jnp.arange(U, dtype=jnp.int32), 'item_indices': jnp.arange(I, dtype=jnp.int32), 'adj_rows': jax.random.randint(ks[0], (NNZ,), 0, N, dtype=jnp.int32), 'adj_cols': jax.random.randint(ks[1], (NNZ,), 0, N, dtype=jnp.int32), 'adj_vals': jax.random.uniform(ks[2], (NNZ,), dtype=jnp.float32), 'user_emb': 0.1 * jax.random.normal(ks[3], (U, D), dtype=jnp.float32), 'item_emb': 0.1 * jax.random.normal(ks[4], (I, D), dtype=jnp.float32), 'gc_W': 0.05 * jax.random.normal(ks[5], (L, D, D), dtype=jnp.float32), 'gc_b': jnp.zeros((L, D), dtype=jnp.float32), 'bi_W': 0.05 * jax.random.normal(ks[6], (L, D, D), dtype=jnp.float32), 'bi_b': jnp.zeros((L, D), dtype=jnp.float32)}
    _L0_rec_all = _L0_rec_setup()
    _L0_rec_in = {k: v for k, v in _L0_rec_all.items() if k in ('item_indices', 'adj_rows', 'adj_cols', 'adj_vals', 'user_emb', 'item_emb', 'gc_W', 'gc_b', 'bi_W', 'bi_b')}
    del _L0_rec_all
    return {'r_user_indices': r_user_indices, 'L0_rec_item_indices': _L0_rec_in['item_indices'], 'L0_rec_adj_rows': _L0_rec_in['adj_rows'], 'L0_rec_adj_cols': _L0_rec_in['adj_cols'], 'L0_rec_adj_vals': _L0_rec_in['adj_vals'], 'L0_rec_user_emb': _L0_rec_in['user_emb'], 'L0_rec_item_emb': _L0_rec_in['item_emb'], 'L0_rec_gc_W': _L0_rec_in['gc_W'], 'L0_rec_gc_b': _L0_rec_in['gc_b'], 'L0_rec_bi_W': _L0_rec_in['bi_W'], 'L0_rec_bi_b': _L0_rec_in['bi_b']}

def reference(r_user_indices, L0_rec_item_indices, L0_rec_adj_rows, L0_rec_adj_cols, L0_rec_adj_vals, L0_rec_user_emb, L0_rec_item_emb, L0_rec_gc_W, L0_rec_gc_b, L0_rec_bi_W, L0_rec_bi_b):
    import jax
    import jax.numpy as jnp

    def _L0_rec_ref(user_indices, item_indices, adj_rows, adj_cols, adj_vals, user_emb, item_emb, gc_W, gc_b, bi_W, bi_b):
        import jax, jax.numpy as jnp
        import numpy as np
        U, I, D, L, NNZ = (1000, 2000, 64, 2, 96000)
        N = U + I
        ego = jnp.concatenate([user_emb[user_indices], item_emb[item_indices]], axis=0)
        n_nodes = ego.shape[0]
        all_embeddings = [ego]
        n_layers = gc_W.shape[0]
        for l in range(n_layers):
            side = jax.ops.segment_sum(adj_vals[:, None] * ego[adj_cols], adj_rows, num_segments=n_nodes)
            sum_emb = jax.nn.leaky_relu(side @ gc_W[l].T + gc_b[l], negative_slope=0.01)
            bi_emb = jax.nn.leaky_relu(ego * side @ bi_W[l].T + bi_b[l], negative_slope=0.01)
            ego = sum_emb + bi_emb
            all_embeddings.append(ego)
        all_emb = jnp.concatenate(all_embeddings, axis=1)
        n_users = user_indices.shape[0]
        u_g = all_emb[:n_users]
        i_g = all_emb[n_users:]
        scores = u_g @ i_g.T
        return jax.nn.log_softmax(scores, axis=1)
    y = _L0_rec_ref(r_user_indices, L0_rec_item_indices, L0_rec_adj_rows, L0_rec_adj_cols, L0_rec_adj_vals, L0_rec_user_emb, L0_rec_item_emb, L0_rec_gc_W, L0_rec_gc_b, L0_rec_bi_W, L0_rec_bi_b)
    return y

_drawn_inputs = setup_inputs


def setup_inputs(seed=0):
    import zlib

    import numpy as np

    out = dict(_drawn_inputs(seed))
    spreads = {'L0_rec_gc_b': (0.0, 0.1), 'L0_rec_bi_b': (0.0, 0.1)}
    factors = {}
    for name, (base, spread) in spreads.items():
        noise = np.random.default_rng([zlib.crc32(name.encode()), seed]).standard_normal(out[name].shape)
        drawn = base * np.exp(spread * noise) if base else spread * noise
        out[name] = jnp.asarray(drawn.astype(out[name].dtype))
    for name, factor in factors.items():
        out[name] = (out[name] * factor).astype(out[name].dtype)
    return out
```

```python
from contextlib import ExitStack

import concourse.bass as bass
from concourse import mybir

ALU = mybir.AluOpType
ACT = mybir.ActivationFunctionType
AX = mybir.AxisListType
F32 = mybir.dt.float32
BF16 = mybir.dt.bfloat16
I32 = mybir.dt.int32
U32 = mybir.dt.uint32

P = 128
NODE_TILE = 125
BANK = 512
CHUNK = 500


def build(nc, user_idx, item_idx, adj_rows, adj_cols, adj_vals, user_emb, item_emb,
          gc_W, gc_b, bi_W, bi_b, out):
    NU = user_idx.shape[0]
    NI = item_idx.shape[0]
    D = user_emb.shape[1]
    L = gc_W.shape[0]
    N = NU + NI
    UT = NU // P
    IT = -(-NI // P)
    GT = UT + IT
    LAST = NI - (IT - 1) * P
    NT = -(-N // NODE_TILE)
    NCOL = NT * NODE_TILE
    EDGES = adj_rows.shape[0]
    ET = EDGES // P
    CH = [(a, min(CHUNK, NCOL - a)) for a in range(0, NCOL, CHUNK)]
    NCH = len(CH)
    TPC = CHUNK // NODE_TILE
    WIDE = 8 * BANK
    assert N <= WIDE and EDGES % P == 0 and 2 * D == P and L == 2

    with ExitStack() as ctx:
        def sb(name, shape, dt=F32):
            return ctx.enter_context(nc.sbuf_tensor(name, shape, dt))

        def sem(name):
            return ctx.enter_context(nc.semaphore(name))

        ps = ctx.enter_context(nc.psum_tensor("ps", [P, 8, BANK], F32))
        table = nc.dram_tensor("ego_table", [NCOL, D], F32, kind="Internal").ap()

        idx = sb("idx", [P, GT], I32)
        ident = sb("ident", [P, P])
        fold = sb("fold", [P, D])
        wblk = sb("wblk", [P, L, P])
        wT = sb("wT", [P, L, P])
        bias = sb("bias", [P, L])
        gath = sb("gath", [P, GT, D])
        emb01 = sb("emb01", [P, NCOL])
        emb2 = sb("emb2", [D, NCOL])
        ego_nm = sb("ego_nm", [P, NT, D])
        stack = sb("stack", [P, NCOL])
        zb = sb("zb", [P, 2, CHUNK])
        lk = sb("lk", [P, 2, CHUNK])

        rows_i = sb("rows_i", [P, ET], I32)
        cols_i = sb("cols_i", [P, ET], I32)
        rv = sb("rv", [P, ET, 2])
        s_col = sb("s_col", [P, 1], I32)
        s_rv = sb("s_rv", [P, 2])
        s_idx = sb("s_idx", [P, 1], I32)
        s_zero = sb("s_zero", [P, 1], I32)
        s_g = sb("s_g", [P, D])
        s_gv = sb("s_gv", [P, D])
        s_iota = sb("s_iota", [P, WIDE])
        s_oh = sb("s_oh", [P, WIDE])

        sc = sb("sc", [P, UT, 5])
        res = sb("res", [P, 2, NI])
        junk = sb("junk", [P, NI], BF16)

        idx_loaded = sem("idx_loaded")
        w_loaded = sem("w_loaded")
        edges_loaded = sem("edges_loaded")
        consts_ready = sem("consts_ready")
        zeroed = sem("zeroed")
        gathered = sem("gathered")
        tr_ready = sem("tr_ready")
        tr_copied = sem("tr_copied")
        rv_ready = sem("rv_ready")
        nm_ready = sem("nm_ready")
        nm_copied = sem("nm_copied")
        table_written = sem("table_written")
        s_staged = sem("s_staged")
        s_gathered = sem("s_gathered")
        s_scaled = sem("s_scaled")
        s_summed = sem("s_summed")
        side_ready = sem("side_ready")
        stack_ready = sem("stack_ready")
        z_ready = sem("z_ready")
        zb_ready = sem("zb_ready")
        lk_ready = sem("lk_ready")
        e_ready = sem("e_ready")
        e_copied = sem("e_copied")
        score_ready = sem("score_ready")
        max_ready = sem("max_ready")
        exp_ready = sem("exp_ready")
        ln_ready = sem("ln_ready")
        shift_ready = sem("shift_ready")
        res_ready = sem("res_ready")
        stored = [sem("stored0"), sem("stored1")]

        block = ctx.enter_context(nc.Block())
        TG = 4
        NTG = GT // TG
        NMG = -(-NT // 8)
        Q = 4
        QC = NI // Q

        @block.sync
        def _(sp):
            with nc.allow_non_contiguous_dma("indices across partitions"):
                sp.dma_start(idx[:, 0:UT], user_idx.rearrange("(t p) -> p t", p=P)).then_inc(idx_loaded, 16)
                sp.dma_start(idx[:, UT:GT - 1], item_idx[0:(IT - 1) * P].rearrange("(t p) -> p t", p=P)).then_inc(idx_loaded, 16)
                sp.dma_start(idx[0:LAST, GT - 1:GT], item_idx[(IT - 1) * P:NI].rearrange("(p a) -> p a", a=1)).then_inc(idx_loaded, 16)
            sp.dma_start(rows_i[:, :], adj_rows.rearrange("(p t) -> p t", p=P)).then_inc(edges_loaded, 16)
            sp.dma_start(cols_i[:, :], adj_cols.rearrange("(p t) -> p t", p=P)).then_inc(edges_loaded, 16)
            with nc.allow_non_contiguous_dma("values next to rows"):
                sp.dma_start(rv[:, :, 1], adj_vals.rearrange("(p t) -> p t", p=P)).then_inc(edges_loaded, 16)
            sp.wait_ge(zeroed, 1)
            for l in range(L):
                sp.dma_start(wblk[0:D, l, 0:D], gc_W[l]).then_inc(w_loaded, 16)
                sp.dma_start(wblk[D:P, l, D:P], bi_W[l]).then_inc(w_loaded, 16)
                sp.dma_start(bias[0:D, l:l + 1], gc_b[l].rearrange("(p a) -> p a", a=1)).then_inc(w_loaded, 16)
                sp.dma_start(bias[D:P, l:l + 1], bi_b[l].rearrange("(p a) -> p a", a=1)).then_inc(w_loaded, 16)
            for l in range(L):
                sp.wait_ge(nm_copied, NMG)
                if l:
                    sp.wait_ge(e_copied, NCH)
                sp.dma_start(table.rearrange("(t p) d -> p t d", p=NODE_TILE), ego_nm[0:NODE_TILE, :, :]).then_inc(table_written, 16)
            for ut in range(UT):
                sp.wait_ge(res_ready, ut + 1)
                sp.dma_start(out[ut * P:(ut + 1) * P, :], res[:, ut % 2, :]).then_inc(stored[ut % 2], 16)
            for s in range(2):
                sp.wait_ge(stored[s], 16 * (UT // 2))

        @block.gpsimd
        def _(pool):
            nc.gpsimd.memset(ident[:, :], 0.0).then_inc(consts_ready, 1)
            nc.gpsimd.memset(fold[:, :], 0.0).then_inc(consts_ready, 1)
            nc.gpsimd.memset(wblk[:, :, :], 0.0).then_inc(zeroed, 1)
            nc.gpsimd.memset(s_zero[:, :], 0)
            pool.wait_ge(consts_ready, 2)
            nc.gpsimd.affine_select(out=ident[:, :], in_=ident[:, :], compare_op=ALU.not_equal, fill=1.0,
                                    base=0, pattern=[[-1, P]], channel_multiplier=1).then_inc(consts_ready, 1)
            nc.gpsimd.affine_select(out=fold[:, :], in_=fold[:, :], compare_op=ALU.not_equal, fill=1.0,
                                    base=0, pattern=[[-1, D]], channel_multiplier=1).then_inc(consts_ready, 1)
            pool.wait_ge(consts_ready, 4)
            nc.gpsimd.affine_select(out=fold[:, :], in_=fold[:, :], compare_op=ALU.not_equal, fill=1.0,
                                    base=-D, pattern=[[-1, D]], channel_multiplier=1).then_inc(consts_ready, 1)
            nc.gpsimd.iota(s_iota[:, :], pattern=[[1, WIDE]], base=0, channel_multiplier=0,
                           allow_small_or_imprecise_dtypes=True).then_inc(consts_ready, 1)
            pool.wait_ge(idx_loaded, 48)
            for t in range(GT):
                n = LAST if t == GT - 1 else P
                src = user_emb if t < UT else item_emb
                nc.gpsimd.indirect_dma_start(
                    gath[0:n, t, :], None, src,
                    bass.IndirectOffsetOnAxis(ap=idx[0:n, t:t + 1].bitcast(U32), axis=0)).then_inc(gathered, 16)

            for l in range(L):
                pool.wait_ge(table_written, 16 * (l + 1))
                with pool.Fori(0, ET) as t:
                    pool.wait_ge(s_staged, t + (l * ET + 1))
                    nc.gpsimd.tensor_tensor(s_idx[:, :], s_col[:, :], s_zero[:, :], ALU.add)
                    nc.gpsimd.drain()
                    nc.gpsimd.indirect_dma_start(
                        s_g[:, :], None, table,
                        bass.IndirectOffsetOnAxis(ap=s_idx[:, :].bitcast(U32), axis=0)).then_inc(s_gathered, 16)

        @block.tensor
        def _(pe):
            pe.wait_ge(consts_ready, 5)
            pe.wait_ge(gathered, 16 * GT)
            for g in range(NTG):
                for i in range(TG):
                    t = g * TG + i
                    n = LAST if t == GT - 1 else P
                    mm = nc.tensor.transpose(ps[0:D, g, i * P:i * P + n], gath[0:n, t, :], ident[0:n, 0:n])
                mm.then_inc(tr_ready, 1)
            pe.wait_ge(w_loaded, 16 * 4 * L)
            for l in range(L):
                pe.wait_ge(tr_copied, l + 1)
                nc.tensor.transpose(ps[:, l, 0:P], wblk[:, l, :], ident[:, :]).then_inc(tr_ready, 1)
            pe.wait_ge(tr_copied, NTG + L)
            for g in range(NMG):
                for i in range(min(8, NT - g * 8)):
                    a = (g * 8 + i) * NODE_TILE
                    mm = nc.tensor.transpose(ps[0:NODE_TILE, g, i * D:(i + 1) * D], emb01[0:D, a:a + NODE_TILE], ident[0:D, 0:D])
                mm.then_inc(nm_ready, 1)

            for l in range(L):
                def sum_tile(first):
                    for b in range(8):
                        mm = nc.tensor.matmul(ps[0:D, b, :], s_gv[:, :], s_oh[:, b * BANK:(b + 1) * BANK],
                                              start=first, stop=True, skip_group_check=True)
                    mm.then_inc(s_summed, 1)
                pe.wait_ge(nm_copied, NMG)
                if l:
                    pe.wait_ge(e_copied, NCH)
                pe.wait_ge(s_scaled, l * ET + 1)
                sum_tile(True)
                with pe.Fori(1, ET) as t:
                    pe.wait_ge(s_scaled, t + (l * ET + 1))
                    sum_tile(False)
                pe.wait_ge(side_ready, l + 1)
                for k, (a, w) in enumerate(CH):
                    n = l * NCH + k
                    pe.wait_ge(stack_ready, n + 1)
                    if n >= 2:
                        pe.wait_ge(zb_ready, n - 1)
                    nc.tensor.matmul(ps[:, k % 2, 0:w], wT[:, l, :], stack[:, a:a + w], start=True, stop=True).then_inc(z_ready, 1)
                    pe.wait_ge(lk_ready, n + 1)
                    if n >= 2:
                        pe.wait_ge(e_copied, n - 1)
                    mm = nc.tensor.matmul(ps[0:D, 2 + k % 2, 0:w], fold[:, :], lk[:, k % 2, 0:w], start=True, stop=True)
                    if l == 0:
                        for i in range(w // NODE_TILE):
                            mm = nc.tensor.matmul(ps[0:NODE_TILE, 4 + k % 2, i * D:(i + 1) * D], lk[:, k % 2, i * NODE_TILE:(i + 1) * NODE_TILE],
                                                  fold[:, :], start=True, stop=True)
                    mm.then_inc(e_ready, 1)
            pe.wait_ge(e_copied, L * NCH)
            for ut in range(UT):
                if ut >= 2:
                    pe.wait_ge(res_ready, ut - 1)
                for q in range(Q):
                    o = ps[:, (ut % 2) * Q + q, 0:QC]
                    u = slice(ut * P, (ut + 1) * P)
                    i = slice(NU + q * QC, NU + (q + 1) * QC)
                    nc.tensor.matmul(o, emb01[:, u], emb01[:, i], start=True, stop=False)
                    mm = nc.tensor.matmul(o, emb2[:, u], emb2[:, i], start=False, stop=True)
                mm.then_inc(score_ready, 1)

        @block.vector
        def _(dve):
            nc.vector.memset(emb01[0:D, N:NCOL], 0.0)
            for g in range(NTG):
                dve.wait_ge(tr_ready, g + 1)
                w = min(TG * P, N - g * TG * P)
                nc.vector.tensor_copy(emb01[0:D, g * TG * P:g * TG * P + w], ps[0:D, g, 0:w]).then_inc(tr_copied, 1)
            for l in range(L):
                dve.wait_ge(tr_ready, NTG + l + 1)
                nc.vector.tensor_copy(wT[:, l, :], ps[:, l, 0:P]).then_inc(tr_copied, 1)
            for g in range(NMG):
                dve.wait_ge(nm_ready, g + 1)
                n = min(8, NT - g * 8)
                nc.vector.tensor_copy(ego_nm[0:NODE_TILE, g * 8:g * 8 + n, :],
                                      ps[0:NODE_TILE, g, 0:n * D].rearrange("p (t d) -> p t d", d=D)).then_inc(nm_copied, 1)
            dve.wait_ge(edges_loaded, 48)
            nc.vector.tensor_copy(rv[:, :, 0], rows_i[:, :]).then_inc(rv_ready, 1)
            dve.wait_ge(rv_ready, 1)
            dve.wait_ge(consts_ready, 6)
            for l in range(L):
                def stage(t, base):
                    if base is not None:
                        dve.wait_ge(s_summed, base)
                    nc.vector.tensor_copy(s_col[:, :], cols_i[:, bass.ds(t, 1)])
                    nc.vector.tensor_copy(s_rv[:, :], rv[:, bass.ds(t, 1), :].rearrange("p a b -> p (a b)")).then_inc(s_staged, 1)

                def scale(n):
                    dve.wait_ge(s_staged, n)
                    nc.vector.tensor_scalar(s_oh[:, :], s_iota[:, :], s_rv[:, 0:1], None, ALU.is_equal)
                    dve.wait_ge(s_gathered, n * 16)
                    nc.vector.tensor_scalar(s_gv[:, :], s_g[:, :], s_rv[:, 1:2], None, ALU.mult).then_inc(s_scaled, 1)

                stage(0, l * ET if l else None)
                scale(l * ET + 1)
                with dve.Fori(1, ET) as t:
                    stage(t, t + l * ET)
                    scale(t + (l * ET + 1))
                dve.wait_ge(s_summed, (l + 1) * ET)
                nc.vector.memset(stack[0:D, N:NCOL], 0.0)
                nc.vector.tensor_copy(stack[0:D, 0:N], ps[0:D, :, :].rearrange("p b c -> p (b c)")[:, 0:N]).then_inc(side_ready, 1)
                dve.wait_ge(side_ready, l + 1)
                ego = emb01 if l == 0 else emb2

                def mult(k):
                    a, w = CH[k]
                    nc.vector.tensor_tensor(stack[D:P, a:a + w], ego[0:D, a:a + w], stack[0:D, a:a + w], ALU.mult).then_inc(stack_ready, 1)
                mult(0)
                for k, (a, w) in enumerate(CH):
                    n = l * NCH + k
                    if k + 1 < NCH:
                        mult(k + 1)
                    dve.wait_ge(zb_ready, n + 1)
                    if n >= 2:
                        dve.wait_ge(e_ready, n - 1)
                    nc.vector.scalar_tensor_tensor(out=lk[:, k % 2, 0:w], in0=zb[:, k % 2, 0:w], scalar=0.01, in1=zb[:, k % 2, 0:w],
                                                   op0=ALU.mult, op1=ALU.max).then_inc(lk_ready, 1)
                    dve.wait_ge(e_ready, n + 1)
                    if l == 0:
                        nc.vector.tensor_copy(emb01[D:P, a:a + w], ps[0:D, 2 + k % 2, 0:w])
                        t0, nt = a // NODE_TILE, w // NODE_TILE
                        nc.vector.tensor_copy(ego_nm[0:NODE_TILE, t0:t0 + nt, :],
                                              ps[0:NODE_TILE, 4 + k % 2, 0:nt * D].rearrange("p (t d) -> p t d", d=D))
                    nc.vector.tensor_copy(emb2[:, a:a + w], ps[0:D, 2 + k % 2, 0:w]).then_inc(e_copied, 1)

            def row_max(ut):
                dve.wait_ge(score_ready, ut + 1)
                nc.vector.tensor_reduce(sc[:, ut, 0:1], ps[:, ut % 2 * Q:ut % 2 * Q + Q, 0:QC], AX.XY, ALU.max).then_inc(max_ready, 1)
                dve.wait_ge(max_ready, 2 * ut + 1)
                nc.vector.tensor_scalar(sc[:, ut, 1:2], sc[:, ut, 0:1], -1.0, None, ALU.mult).then_inc(max_ready, 1)

            def subtract(ut):
                dve.wait_ge(ln_ready, ut + 1)
                nc.vector.tensor_tensor(sc[:, ut, 4:5], sc[:, ut, 0:1], sc[:, ut, 3:4], ALU.add).then_inc(shift_ready, 1)
                dve.wait_ge(shift_ready, ut + 1)
                if ut >= 2:
                    dve.wait_ge(stored[ut % 2], 16 * (ut // 2))
                nc.vector.tensor_scalar(res[:, ut % 2, :].rearrange("p (q c) -> p q c", q=Q), ps[:, ut % 2 * Q:ut % 2 * Q + Q, 0:QC],
                                        sc[:, ut, 4:5], None, ALU.subtract).then_inc(res_ready, 1)

            for ut in range(UT):
                row_max(ut)
                if ut:
                    subtract(ut - 1)
            subtract(UT - 1)

        @block.scalar
        def _(act):
            for l in range(L):
                for k, (a, w) in enumerate(CH):
                    n = l * NCH + k
                    act.wait_ge(z_ready, n + 1)
                    if n >= 2:
                        act.wait_ge(lk_ready, n - 1)
                    nc.scalar.activation(zb[:, k % 2, 0:w], ps[:, k % 2, 0:w], ACT.Identity, bias=bias[:, l:l + 1]).then_inc(zb_ready, 1)
            for ut in range(UT):
                act.wait_ge(max_ready, 2 * ut + 2)
                if ut:
                    act.wait_ge(exp_ready, ut)
                nc.scalar.activation(junk[:, :].rearrange("p (q c) -> p q c", q=Q), ps[:, ut % 2 * Q:ut % 2 * Q + Q, 0:QC], ACT.Exp,
                                     bias=sc[:, ut, 1:2], accum_out=sc[:, ut, 2:3]).then_inc(exp_ready, 1)
                act.wait_ge(exp_ready, ut + 1)
                nc.scalar.activation(sc[:, ut, 3:4], sc[:, ut, 2:3], ACT.Ln).then_inc(ln_ready, 1)


_INS = ["r_user_indices", "L0_rec_item_indices", "L0_rec_adj_rows", "L0_rec_adj_cols", "L0_rec_adj_vals",
        "L0_rec_user_emb", "L0_rec_item_emb", "L0_rec_gc_W", "L0_rec_gc_b", "L0_rec_bi_W", "L0_rec_bi_b"]


def kernel(**inputs):
    import numpy as np
    import concourse.bacc as bacc
    from concourse.bass_utils import run_bass_kernel_spmd

    nc = bacc.Bacc("TRN2", target_bir_lowering=False, num_devices=1)
    arrays, args = {}, []
    for name in _INS:
        a = np.ascontiguousarray(inputs[name])
        arrays[f"in_{name}"] = a
        args.append(nc.dram_tensor(f"in_{name}", a.shape, mybir.dt.from_np(a.dtype), kind="ExternalInput").ap())
    shape = (inputs["r_user_indices"].shape[0], inputs["L0_rec_item_indices"].shape[0])
    args.append(nc.dram_tensor("out_scores", shape, F32, kind="ExternalOutput").ap())
    build(nc, *args)
    r = run_bass_kernel_spmd(nc, [arrays], core_ids=[0])
    return r.results[0]["out_scores"]
```

```python
from contextlib import ExitStack

import concourse.bass as bass
from concourse import mybir

ALU = mybir.AluOpType
ACT = mybir.ActivationFunctionType
AX = mybir.AxisListType
F32 = mybir.dt.float32
BF16 = mybir.dt.bfloat16
I32 = mybir.dt.int32
U32 = mybir.dt.uint32

P = 128
BANK = 512
BATCH = 16
ROUND = 12582912.0
BIG = 8193.0
CB = 125
RB = 60
CHUNK = 500


def build(nc, user_idx, item_idx, adj_rows, adj_cols, adj_vals, user_emb, item_emb,
          gc_W, gc_b, bi_W, bi_b, out):
    NU, NI = user_idx.shape[0], item_idx.shape[0]
    D = user_emb.shape[1]
    L = gc_W.shape[0]
    N = NU + NI
    GRAPH = user_emb.shape[0] + item_emb.shape[0]
    UT = NU // P
    IT = -(-NI // P)
    GT = UT + IT
    LAST = NI - (IT - 1) * P
    NT = -(-N // CB)
    NCOL = NT * CB
    ET = adj_rows.shape[0] // P
    NB1 = GRAPH // CB
    NB2 = GRAPH // RB
    NBATCH = -(-ET // BATCH)
    EP = NBATCH * BATCH
    THIRDS = -(-NBATCH // BATCH)
    SLOTS = THIRDS * BATCH
    GW = 8
    NG = -(-NB2 // GW)
    GROUPS = [(a, min(GW, NB2 - a)) for a in range(0, NB2, GW)]
    F1 = 6
    F2 = F1 - 1
    SQ = GRAPH // CHUNK
    HALF_BANK = GW
    HELD = 4
    SPILLED = NB1 - 2 - HELD
    CH = [(a, min(CHUNK, NCOL - a)) for a in range(0, NCOL, CHUNK)]
    NCH = len(CH)
    Q = 4
    QC = NI // Q
    TG = 4
    NTG = GT // TG
    NMG = -(-NT // GW)
    OB = 8
    assert 2 * D == P and L == 2 and GRAPH == NB1 * CB == NB2 * RB and N <= OB * BANK
    assert NBATCH % 2 == 1 and NB1 % 2 == 0 and SLOTS > NBATCH and SPILLED % 2 == 0

    with ExitStack() as ctx:
        def sb(name, shape, dt=F32):
            return ctx.enter_context(nc.sbuf_tensor(name, shape, dt))

        def sem(name):
            return ctx.enter_context(nc.semaphore(name))

        class Arena:

            def __init__(self, name, words):
                self.mem, self.at, self.words = sb(name, [P, words]), 0, words

            def take(self, shape, dt=F32):
                n = 1
                for s in shape:
                    n *= s
                w = n if dt in (F32, I32) else -(-n // 2)
                v = self.mem[:, self.at:self.at + w]
                self.at += w
                assert self.at <= self.words, (self.at, self.words)
                if dt != F32:
                    v = v.bitcast(dt)[:, 0:n]
                names = "abcd"[:len(shape)]
                if len(shape) > 1:
                    v = v.rearrange(f"p ({' '.join(names)}) -> p {' '.join(names)}", **dict(zip(names, shape)))
                return v

            def reuse(self):
                self.at = 0

        ps = ctx.enter_context(nc.psum_tensor("ps", [P, 8, BANK], F32))
        spill = nc.dram_tensor("spilled_blocks", [SPILLED, P, GRAPH], F32, kind="Internal").ap()
        table = nc.dram_tensor("ego_table", [NCOL, D], F32, kind="Internal").ap()

        idx = sb("idx", [P, GT], I32)
        ident = sb("ident", [P, P])
        fold = sb("fold", [P, D])
        wblk = sb("wblk", [P, L, P])
        wT = sb("wT", [P, L, P])
        bias = sb("bias", [P, L])
        emb01 = sb("emb01", [P, NCOL])
        ego_nm = sb("ego_nm", [P, NT, D])
        ones = sb("ones", [P, P], BF16)
        count = sb("count", [P, P], BF16)
        zeros = sb("zeros", [P, BANK], BF16)
        iota_s = sb("iota_s", [P, P, BATCH], BF16)
        iota_1 = sb("iota_1", [P, NB1, BATCH], BF16)
        mask_1 = sb("mask_1", [P, NB1, BATCH], BF16)
        iota_2 = sb("iota_2", [P, NB2, SLOTS], BF16)
        mask_2 = sb("mask_2", [P, NB2, SLOTS], BF16)
        rows_i = sb("rows_i", [P, ET], I32)
        cols_i = sb("cols_i", [P, ET], I32)
        rv = sb("rv", [P, ET, 2])
        rank1 = sb("rank1", [P, EP], BF16)
        rank2 = sb("rank2", [P, NB1, SLOTS], BF16)
        rk = sb("rk", [P, 2, BATCH])
        lhs = sb("lhs", [P, 2, D])
        worst = sb("worst", [P, 4])
        over = sb("over", [P, 3])
        flag = sb("flag", [1, 1], I32)
        one_f = sb("one_f", [P, 1])
        work = sb("work", [P, 2, GRAPH])
        s_col = sb("s_col", [P, 1], I32)
        s_idx = sb("s_idx", [P, 1], I32)
        s_zero = sb("s_zero", [P, 1], I32)
        s_rv = sb("s_rv", [P, 2])
        s_g = sb("s_g", [P, D])
        s_gv = sb("s_gv", [P, D])
        sc = sb("sc", [P, UT, 5])

        held_mem = Arena("held_mem", HELD * GRAPH)
        held = held_mem.take([HELD, GRAPH])
        held_mem.reuse()
        gath = held_mem.take([GT, D])
        colf, t0, t1 = (held_mem.take([ET]) for _ in range(3))
        cbin = held_mem.take([EP], BF16)
        pay = held_mem.take([F1, EP], BF16)

        work_mem = Arena("work_mem", 17300)
        slots1 = work_mem.take([NB1, F1, SLOTS], BF16)
        onehot_slot = work_mem.take([2, P, BATCH], BF16)
        spread = work_mem.take([2, NB2 * F2, BATCH], BF16)
        bins2 = work_mem.take([2, NB2, SLOTS], BF16)
        scan2 = work_mem.take([NB2, SLOTS], BF16)
        slots2 = work_mem.take([2, F2, NB2], BF16)
        onehot_c = work_mem.take([2, P, GW], BF16)
        onehot_r = work_mem.take([2, RB, GW], BF16)
        valued = work_mem.take([2, RB, 3, GW], BF16)
        bins1 = bins2.rearrange("p a b c -> p (a b c)")[:, 0:2 * NB1 * BATCH].rearrange("p (a b c) -> p a b c", a=2, b=NB1)
        scan1 = scan2.rearrange("p b c -> p (b c)")[:, 0:2 * NB1 * BATCH].rearrange("p (a b c) -> p a b c", a=2, b=NB1)
        spread1 = spread[:, :, 0:NB1 * F1, :]
        work_mem.reuse()
        stack = work_mem.take([NCOL])
        emb2 = work_mem.take([NCOL])
        late = work_mem.take([2, GRAPH])
        zb = sb("zb", [P, 2, CHUNK])
        lk = sb("lk", [P, 2, BANK])
        s_iota = zb[:, :, :].rearrange("p a b -> p (a b)")[:, 0:BANK]
        res = work
        junk = held_mem.mem[:, 0:NI // 2].bitcast(BF16)

        names = """idx_loaded w_loaded edges_loaded consts_ready zeroed pool_ready gathered prep_done
            l1_bins rank_rounded l1_rank l1_rank_read l1_slots l1_scattered l1_stored
            tr_ready tr_copied nm_ready nm_copied pads_zeroed
            l2_bins l2_rank l2_rank_read l2_slots l2_scattered l2_stored
            l3_onehot l3_ready l3_built l3_stored lhs_ready side_zeroed side_added
            flag_parts flag_vec flag_sum flag_ready table_written
            s_counted s_staged s_gathered s_scaled s_onehot s_summed s_side
            stack_zeroed side_ready stack_ready z_ready zb_ready lk_ready e_ready e_copied nm2_copied
            score_ready max_ready exp_ready ln_ready shift_ready res_ready""".split()
        S = {n: sem(n) for n in names}
        stored_out = [sem("stored_out0"), sem("stored_out1")]
        block_saved = [sem("block_saved0"), sem("block_saved1")]
        NSLOT = 2 + HELD + 2
        block_back = [sem(f"block_back{i}") for i in range(NSLOT)]

        ORDER = [NB1 - 2, NB1 - 1] + list(range(SPILLED, NB1 - 2)) + list(range(SPILLED))
        NRES = 2 + HELD

        def ring(i):
            s = i % NSLOT
            if s < 2:
                return work[:, s, :]
            if s < NRES:
                return held[:, s - 2, :]
            return late[:, s - NRES, :]

        def side_piece(q):
            return ps[(q % 2) * D:(q % 2) * D + D, q // 2, 0:CHUNK]

        def at(x, k=1):
            return bass.ds(x, k)

        block = ctx.enter_context(nc.Block())

        @block.sync
        def _(sp):
            with nc.allow_non_contiguous_dma("small loads across partitions"):
                sp.dma_start(cols_i[:, :], adj_cols.rearrange("(p t) -> p t", p=P)).then_inc(S["edges_loaded"], 16)
                sp.dma_start(rows_i[:, :], adj_rows.rearrange("(p t) -> p t", p=P)).then_inc(S["edges_loaded"], 16)
                sp.dma_start(t1[:, :], adj_vals.rearrange("(p t) -> p t", p=P)).then_inc(S["edges_loaded"], 16)
                sp.dma_start(idx[:, 0:UT], user_idx.rearrange("(t p) -> p t", p=P)).then_inc(S["idx_loaded"], 16)
                sp.dma_start(idx[:, UT:GT - 1], item_idx[0:(IT - 1) * P].rearrange("(t p) -> p t", p=P)).then_inc(S["idx_loaded"], 16)
                sp.dma_start(idx[0:LAST, GT - 1:GT], item_idx[(IT - 1) * P:NI].rearrange("(p a) -> p a", a=1)).then_inc(S["idx_loaded"], 16)
                sp.wait_ge(S["zeroed"], 1)
                for l in range(L):
                    sp.dma_start(wblk[0:D, l, 0:D], gc_W[l]).then_inc(S["w_loaded"], 16)
                    sp.dma_start(wblk[D:P, l, D:P], bi_W[l]).then_inc(S["w_loaded"], 16)
                    sp.dma_start(bias[0:D, l:l + 1], gc_b[l].rearrange("(p a) -> p a", a=1)).then_inc(S["w_loaded"], 16)
                    sp.dma_start(bias[D:P, l:l + 1], bi_b[l].rearrange("(p a) -> p a", a=1)).then_inc(S["w_loaded"], 16)

            with sp.Fori(0, (SPILLED) // 2) as pair:
                k = 2 * pair
                for j in range(2):
                    sp.wait_ge(S["l3_stored"], k * NG + NG * (j + 1))
                    sp.dma_start(spill[at(k + j), :, :].rearrange("a p c -> p (a c)"), work[:, j, :]).then_inc(block_saved[j], 16)
            for k in range(SPILLED, NB1 - 2):
                sp.wait_ge(S["l3_stored"], NG * (k + 1))
                sp.dma_start(held[:, k - SPILLED, :], work[:, k % 2, :]).then_inc(block_saved[k % 2], 16)

            def bring_back(i):
                if i >= NRES and i < NSLOT:
                    sp.wait_ge(S["l3_built"], NB1 * NG)
                if i >= NSLOT:
                    sp.wait_ge(S["side_added"], NB1 + 1 + i - NSLOT)
                sp.dma_start(ring(i), spill[ORDER[i]]).then_inc(block_back[i % NSLOT], 16)

            for j in range(2):
                sp.wait_ge(block_saved[j], 16 * (NB1 // 2 - 1))
            for i in range(NRES, NSLOT):
                bring_back(i)

            def fallback(l):
                sp.wait_ge(S["nm_copied"], NMG)
                if l:
                    sp.wait_ge(S["nm2_copied"], NCH)
                sp.dma_start(table.rearrange("(t p) d -> p t d", p=CB), ego_nm[0:CB, :, :]).then_inc(S["table_written"], 16)

            sp.wait_ge(S["flag_ready"], 1)
            overflow = sp.value_load(flag[0:1, 0:1])
            with sp.If(overflow):
                fallback(0)
            for i in range(NSLOT, NB1):
                bring_back(i)
            with sp.If(overflow):
                fallback(1)
            for ut in range(UT):
                sp.wait_ge(S["res_ready"], ut + 1)
                sp.dma_start(out[ut * P:(ut + 1) * P, :], res[:, ut % 2, 0:NI]).then_inc(stored_out[ut % 2], 16)
            for s in range(2):
                sp.wait_ge(stored_out[s], 16 * (UT // 2))

        @block.gpsimd
        def _(pool):
            ready = S["consts_ready"]
            nc.gpsimd.memset(ones[:, :], 1.0)
            nc.gpsimd.memset(count[:, :], -1.0)
            nc.gpsimd.memset(ident[:, :], 0.0)
            nc.gpsimd.memset(fold[:, :], 0.0)
            nc.gpsimd.memset(s_zero[:, :], 0)
            nc.gpsimd.memset(zeros[:, :], 0.0)
            nc.gpsimd.memset(one_f[:, :], 1.0)
            nc.gpsimd.memset(mask_1[:, :, :], 1.0)
            nc.gpsimd.memset(wblk[:, :, :], 0.0).then_inc(S["zeroed"], 1)
            pool.wait_ge(S["zeroed"], 1)
            nc.gpsimd.memset(mask_1[:, :, 0:1], 0.0)
            nc.gpsimd.affine_select(out=count[:, :], in_=count[:, :], compare_op=ALU.is_ge, fill=0.0,
                                    base=0, pattern=[[-1, P]], channel_multiplier=1)
            nc.gpsimd.iota(iota_1[:, :, :], pattern=[[1, NB1], [0, BATCH]], base=0, channel_multiplier=0,
                           allow_small_or_imprecise_dtypes=True)
            nc.gpsimd.iota(iota_s[:, :, :], pattern=[[1, P], [0, BATCH]], base=0, channel_multiplier=0,
                           allow_small_or_imprecise_dtypes=True).then_inc(ready, 1)
            pool.wait_ge(ready, 1)
            nc.gpsimd.affine_select(out=count[:, :], in_=count[:, :], compare_op=ALU.not_equal, fill=BIG - 1,
                                    base=0, pattern=[[-1, P]], channel_multiplier=1).then_inc(ready, 1)
            nc.gpsimd.memset(mask_2[:, :, :], 1.0)
            nc.gpsimd.affine_select(out=ident[:, :], in_=ident[:, :], compare_op=ALU.not_equal, fill=1.0,
                                    base=0, pattern=[[-1, P]], channel_multiplier=1)
            nc.gpsimd.affine_select(out=fold[:, :], in_=fold[:, :], compare_op=ALU.not_equal, fill=1.0,
                                    base=0, pattern=[[-1, D]], channel_multiplier=1).then_inc(ready, 1)
            pool.wait_ge(ready, 3)
            nc.gpsimd.memset(mask_2[:, :, 0:1], 0.0)
            nc.gpsimd.affine_select(out=fold[:, :], in_=fold[:, :], compare_op=ALU.not_equal, fill=1.0,
                                    base=-D, pattern=[[-1, D]], channel_multiplier=1)
            nc.gpsimd.iota(iota_2[:, :, :], pattern=[[1, NB2], [0, SLOTS]], base=1, channel_multiplier=0,
                           allow_small_or_imprecise_dtypes=True).then_inc(ready, 1)
            pool.wait_ge(S["idx_loaded"], 48)
            for t in range(GT):
                n = LAST if t == GT - 1 else P
                src = user_emb if t < UT else item_emb
                nc.gpsimd.indirect_dma_start(
                    gath[0:n, t, :], None, src,
                    bass.IndirectOffsetOnAxis(ap=idx[0:n, t:t + 1].bitcast(U32), axis=0)).then_inc(S["gathered"], 16)

            def hand_over(k, j):
                nc.gpsimd.tensor_copy(lhs[0:CB, j, :], ego_nm[0:CB, at(k), :].rearrange("p a d -> p (a d)")).then_inc(S["lhs_ready"], 1)
            pool.wait_ge(S["nm_copied"], NMG)
            hand_over(0, 0)
            hand_over(1, 1)
            with pool.Fori(1, (NB1) // 2) as pair:
                k = 2 * pair
                for j in range(2):
                    pool.wait_ge(S["side_added"], k + (j - 1))
                    hand_over(k + j, j)

            def fallback(l):
                if l:
                    pool.wait_ge(S["lk_ready"], l * NCH)
                nc.gpsimd.iota(s_iota, pattern=[[1, BANK]], base=0, channel_multiplier=0,
                               allow_small_or_imprecise_dtypes=True).then_inc(S["s_counted"], 1)
                pool.wait_ge(S["table_written"], 16 * (l + 1))
                with pool.Fori(0, ET) as t:
                    pool.wait_ge(S["s_staged"], t + (l * ET + 1))
                    nc.gpsimd.tensor_tensor(s_idx[:, :], s_col[:, :], s_zero[:, :], ALU.add)
                    nc.gpsimd.drain()
                    nc.gpsimd.indirect_dma_start(
                        s_g[:, :], None, table,
                        bass.IndirectOffsetOnAxis(ap=s_idx[:, :].bitcast(U32), axis=0)).then_inc(S["s_gathered"], 16)

            pool.wait_ge(S["flag_ready"], 1)
            overflow = pool.value_load(flag[0:1, 0:1])
            with pool.If(overflow):
                fallback(0)
                fallback(1)

        @block.tensor
        def _(pe):
            mm = nc.tensor.matmul

            def rank1_of(m, j):
                pe.wait_ge(S["l1_bins"], 2 * m + 2)
                flat = lambda x: x.rearrange("p b c -> p (b c)")
                if isinstance(m, int):
                    if m >= 2:
                        pe.wait_ge(S["l1_rank_read"], m - 1)
                else:
                    pe.wait_ge(S["l1_rank_read"], m - 1)
                mm(ps[:, 4 + j, 0:NB1 * BATCH], ones[:, :], flat(scan1[:, j]), start=True, stop=False)
                mm(ps[:, 4 + j, 0:NB1 * BATCH], count[:, :], flat(bins1[:, j]), start=False, stop=True).then_inc(S["l1_rank"], 1)

            def scatter1(m, j, first=False):
                pe.wait_ge(S["l1_slots"], m + 1)
                if not first:
                    pe.wait_ge(S["l1_stored"], m - 1)
                for t in range(BATCH):
                    x = mm(ps[:, 6 + j, 0:NB1 * F1], onehot_slot[:, j, :, t], spread1[:, j, :, t], start=(t == 0), stop=(t == BATCH - 1))
                x.then_inc(S["l1_scattered"], 1)

            pe.wait_ge(S["consts_ready"], 2)
            rank1_of(0, 0)
            rank1_of(1, 1)
            scatter1(0, 0, True)
            rank1_of(2, 0)
            scatter1(1, 1, True)
            with pe.Fori(1, (NBATCH - 1) // 2) as pair:
                m = 2 * pair
                rank1_of(m + 1, 1)
                scatter1(m, 0)
                rank1_of(m + 2, 0)
                scatter1(m + 1, 1)
            scatter1(NBATCH - 1, 0)

            pe.wait_ge(S["consts_ready"], 4)
            pe.wait_ge(S["gathered"], 16 * GT)
            pe.wait_ge(S["l1_stored"], NBATCH)
            pe.wait_ge(S["l1_rank_read"], NBATCH)
            for g in range(NTG):
                for i in range(TG):
                    t = g * TG + i
                    n = LAST if t == GT - 1 else P
                    x = nc.tensor.transpose(ps[0:D, g, i * P:i * P + n], gath[0:n, t, :], ident[0:n, 0:n])
                x.then_inc(S["tr_ready"], 1)
            pe.wait_ge(S["w_loaded"], 16 * 4 * L)
            for l in range(L):
                pe.wait_ge(S["tr_copied"], l + 1)
                nc.tensor.transpose(ps[:, l, 0:P], wblk[:, l, :], ident[:, :]).then_inc(S["tr_ready"], 1)
            pe.wait_ge(S["tr_copied"], NTG + L)
            for g in range(NMG):
                for i in range(min(GW, NT - g * GW)):
                    a = (g * GW + i) * CB
                    x = nc.tensor.transpose(ps[0:CB, g, i * D:(i + 1) * D], emb01[0:D, a:a + CB], ident[0:D, 0:D])
                x.then_inc(S["nm_ready"], 1)
            pe.wait_ge(S["nm_copied"], NMG)

            def rank2_of(c, j, h, first=False):
                if h == 0:
                    pe.wait_ge(S["l2_bins"], 2 * c + 2)
                if not (first and h == 0):
                    pe.wait_ge(S["l2_rank_read"], THIRDS * c + h)
                for b in range(BATCH // HALF_BANK):
                    s = slice(h * BATCH + b * HALF_BANK, h * BATCH + (b + 1) * HALF_BANK)
                    o = ps[:, 4 + b, 0:NB2 * HALF_BANK].rearrange("p (b c) -> p b c", b=NB2)
                    mm(o, ones[:, :], scan2[:, :, s], start=True, stop=False)
                    x = mm(o, count[:, :], bins2[:, j, :, s], start=False, stop=True)
                x.then_inc(S["l2_rank"], 1)

            def scatter2(c, j, h, first=False):
                pe.wait_ge(S["l2_slots"], THIRDS * c + (h + 1))
                if h == 0 and not first:
                    pe.wait_ge(S["l2_stored"], c)
                w = (j + h) % 2
                for t in range(BATCH):
                    x = mm(ps[:, 3, 0:NB2 * F2], onehot_slot[:, w, :, t], spread[:, w, :, t],
                           start=(h == 0 and t == 0), stop=(h == THIRDS - 1 and t == BATCH - 1))
                x.then_inc(S["l2_scattered"], 1)

            def level3(k, j, g, early):
                a, n = GROUPS[g]
                w = (j + g) % 2
                pe.wait_ge(S["l3_ready"], k * NG + (g + 1))
                if not (early and g < 2):
                    pe.wait_ge(S["l3_stored"], k * NG + (g - 1))
                for b in range(n):
                    for v in range(3):
                        x = mm(ps[:, 6 + w, b * RB:(b + 1) * RB], onehot_c[:, w, :, b], valued[:, w, :, v, b],
                               start=(v == 0), stop=(v == 2))
                x.then_inc(S["l3_built"], 1)

            def add_side(k, j):
                pe.wait_ge(S["l3_stored"], (k + 1) * NG)
                pe.wait_ge(S["lhs_ready"], k + 1)
                for q in range(SQ):
                    x = mm(side_piece(q), lhs[0:CB, j, :], work[0:CB, j, q * CHUNK:(q + 1) * CHUNK],
                           start=False, stop=True, skip_group_check=True)
                x.then_inc(S["side_added"], 1)

            def step(c, j, l2=True, l3=True, add=True, first=False):
                if l2:
                    rank2_of(c, j, 0, first)
                for h in range(THIRDS):
                    if l3:
                        for g in range(h * 2, min(h * 2 + 2, NG) if h < THIRDS - 1 else NG):
                            level3(c - 1, 1 - j, g, first or (isinstance(c, int) and c == 1))
                    if l2:
                        scatter2(c, j, h, first)
                        if h + 1 < THIRDS:
                            rank2_of(c, j, h + 1, first)
                    if h == 0 and add:
                        add_side(c - 2, j)

            for q in range(SQ):
                mm(side_piece(q), zeros[:, 0:D], zeros[:, 0:CHUNK], start=True, stop=True)
            step(0, 0, l3=False, add=False, first=True)
            step(1, 1, add=False)
            with pe.Fori(1, (NB1) // 2) as pair:
                c = 2 * pair
                step(c, 0)
                step(c + 1, 1)
            step(NB1, 0, l2=False)
            step(NB1 + 1, 1, l2=False, l3=False)

            pe.wait_ge(S["flag_vec"], 1)
            pe.wait_ge(S["l3_stored"], NB1 * NG)
            mm(ps[0:1, 6, 0:1], over[:, 2:3], one_f[:, :], start=True, stop=True).then_inc(S["flag_sum"], 1)
            pe.wait_ge(S["flag_ready"], 1)
            overflow = pe.value_load(flag[0:1, 0:1])

            def fallback(l):
                pe.wait_ge(S["side_ready"], (l + 1) * SQ)

                def add_tile(t, first):
                    for b in range(OB):
                        pe.wait_ge(S["s_onehot"], t * OB + (l * ET * OB + b + 1))
                        if b == 0:
                            pe.wait_ge(S["s_scaled"], t + (l * ET + 1))
                        mm(ps[0:D, b, :], s_gv[:, :], lk[:, b % 2, :], start=first, stop=True,
                           skip_group_check=True).then_inc(S["s_summed"], 1)
                add_tile(0, True)
                with pe.Fori(1, ET) as t:
                    add_tile(t, False)
                pe.wait_ge(S["s_side"], l + 1)

            for l in range(L):
                if l:
                    pe.wait_ge(S["nm2_copied"], NCH)
                    pe.wait_ge(S["side_ready"], l * SQ)
                    for j in range(2):
                        pe.wait_ge(block_saved[j], 16 * (NB1 // 2 - 1))
                    for q in range(SQ):
                        mm(side_piece(q), zeros[:, 0:D], zeros[:, 0:CHUNK], start=True, stop=True)
                    for i, k in enumerate(ORDER):
                        if i >= NRES:
                            pe.wait_ge(block_back[i % NSLOT], 16 * (i // NSLOT + (i % NSLOT >= NRES)))
                        for q in range(SQ):
                            x = mm(side_piece(q), ego_nm[0:CB, k, :], ring(i)[0:CB, q * CHUNK:(q + 1) * CHUNK],
                                   start=False, stop=True, skip_group_check=True)
                        x.then_inc(S["side_added"], 1)
                with pe.If(overflow):
                    fallback(l)
                for k, (a, w) in enumerate(CH):
                    n = l * NCH + k
                    pe.wait_ge(S["stack_ready"], n + 1)
                    if n >= 2:
                        pe.wait_ge(S["zb_ready"], n - 1)
                    mm(ps[:, 4 + k % 2, 0:w], wT[:, l, :], stack[:, a:a + w], start=True, stop=True).then_inc(S["z_ready"], 1)
                    pe.wait_ge(S["lk_ready"], n + 1)
                    if n >= 2:
                        pe.wait_ge(S["e_copied"], n - 1)
                    x = mm(ps[0:D, 6 + k % 2, 0:w], fold[:, :], lk[:, k % 2, 0:w], start=True, stop=True)
                    if l == 0:
                        if k >= 1:
                            pe.wait_ge(S["nm2_copied"], k)
                        for i in range(w // CB):
                            x = mm(ps[0:CB, 3, i * D:(i + 1) * D], lk[:, k % 2, i * CB:(i + 1) * CB], fold[:, :], start=True, stop=True)
                    x.then_inc(S["e_ready"], 1)
            pe.wait_ge(S["e_copied"], L * NCH)
            for ut in range(UT):
                if ut >= 2:
                    pe.wait_ge(S["res_ready"], ut - 1)
                for q in range(Q):
                    o = ps[:, (ut % 2) * Q + q, 0:QC]
                    u = slice(ut * P, (ut + 1) * P)
                    i = slice(NU + q * QC, NU + (q + 1) * QC)
                    mm(o, emb01[:, u], emb01[:, i], start=True, stop=False)
                    x = mm(o, emb2[0:D, u], emb2[0:D, i], start=False, stop=True)
                x.then_inc(S["score_ready"], 1)

        @block.vector
        def _(dve):
            v = nc.vector
            done = [0]

            def chain(ins):
                done[0] += 1
                ins.then_inc(S["prep_done"], 1)
                dve.wait_ge(S["prep_done"], done[0])

            v.memset(emb01[0:D, N:NCOL], 0.0)
            v.memset(slots1[:, :, :, NBATCH:SLOTS], 0.0)
            v.memset(cbin[:, ET:EP], 255.0)
            v.memset(pay[:, :, ET:EP], 0.0).then_inc(S["pads_zeroed"], 1)
            dve.wait_ge(S["edges_loaded"], 48)
            v.tensor_copy(colf, cols_i[:, :])
            v.tensor_copy(rv[:, :, 0], rows_i[:, :])
            v.tensor_copy(pay[:, 3, 0:ET], t1)
            chain(v.tensor_copy(rv[:, :, 1], t1))
            v.tensor_reduce(worst[:, 2:3], colf, AX.X, ALU.max)
            v.tensor_reduce(worst[:, 3:4], rv[:, :, 0], AX.X, ALU.max)
            chain(v.tensor_scalar(t0, colf, 1.0 / CB, 0.5 / CB - 0.5, ALU.mult, ALU.add))
            chain(v.tensor_scalar(t0, t0, ROUND, ROUND, ALU.add, ALU.subtract))
            v.tensor_copy(cbin[:, 0:ET], t0)
            chain(v.scalar_tensor_tensor(out=pay[:, 1, 0:ET], in0=t0, scalar=-float(CB), in1=colf, op0=ALU.mult, op1=ALU.add))
            chain(v.tensor_scalar(colf, rv[:, :, 0], 1.0 / RB, 0.5 / RB - 0.5, ALU.mult, ALU.add))
            chain(v.tensor_scalar(colf, colf, ROUND, ROUND, ALU.add, ALU.subtract))
            v.tensor_scalar(pay[:, 0, 0:ET], colf, 1.0, None, ALU.add)
            v.scalar_tensor_tensor(out=pay[:, 2, 0:ET], in0=colf, scalar=-float(RB), in1=rv[:, :, 0], op0=ALU.mult, op1=ALU.add)
            chain(v.tensor_tensor(t0, t1, pay[:, 3, 0:ET], ALU.subtract))
            chain(v.tensor_copy(pay[:, 4, 0:ET], t0))
            chain(v.tensor_tensor(t0, t0, pay[:, 4, 0:ET], ALU.subtract))
            chain(v.tensor_copy(pay[:, 5, 0:ET], t0))
            dve.wait_ge(S["consts_ready"], 1)

            def batch(m, k=1):
                return bass.ds(m * BATCH, k * BATCH)

            def along(x, shape, axis):
                return x.unsqueeze(axis).to_broadcast(shape)

            def bins_of(m, j):
                v.tensor_tensor(bins1[:, j], iota_1[:, :, :], along(cbin[:, batch(m)], [P, NB1, BATCH], 1), ALU.is_equal).then_inc(S["l1_bins"], 1)
                dve.wait_ge(S["l1_bins"], 2 * m + 1)
                v.tensor_tensor_scan(scan1[:, j].rearrange("p b c -> p (b c)"), mask_1[:, :, :].rearrange("p b c -> p (b c)"),
                                     bins1[:, j].rearrange("p b c -> p (b c)"), 0.0, ALU.mult, ALU.add).then_inc(S["l1_bins"], 1)

            def slots_of(m, j, early=False):
                if not early:
                    dve.wait_ge(S["l1_scattered"], m - 1)
                v.tensor_tensor(spread1[:, j].rearrange("p (b f) c -> p b f c", f=F1),
                                along(bins1[:, j], [P, NB1, F1, BATCH], 2), along(pay[:, :, batch(m)], [P, NB1, F1, BATCH], 1), ALU.mult)
                dve.wait_ge(S["l1_rank"], m + 1)
                v.tensor_reduce(rk[:, j, :], ps[:, 4 + j, 0:NB1 * BATCH].rearrange("p (b c) -> p c b", c=BATCH),
                                AX.X, ALU.max).then_inc(S["l1_rank_read"], 1)
                dve.wait_ge(S["l1_rank_read"], m + 1)
                v.tensor_scalar(rank1[:, batch(m)], rk[:, j, :], -BIG, None, ALU.add).then_inc(S["rank_rounded"], 1)
                dve.wait_ge(S["rank_rounded"], m + 1)
                v.tensor_tensor(onehot_slot[:, j], iota_s[:, :, :], along(rank1[:, batch(m)], [P, P, BATCH], 1), ALU.is_equal).then_inc(S["l1_slots"], 1)

            bins_of(0, 0)
            bins_of(1, 1)
            slots_of(0, 0, True)
            bins_of(2, 0)
            slots_of(1, 1, True)
            with dve.Fori(1, (NBATCH - 1) // 2) as pair:
                m = 2 * pair
                bins_of(m + 1, 1)
                slots_of(m, 0)
                bins_of(m + 2, 0)
                slots_of(m + 1, 1)
            slots_of(NBATCH - 1, 0)

            dve.wait_ge(S["consts_ready"], 4)
            dve.wait_ge(S["l1_stored"], NBATCH)
            dve.wait_ge(S["l1_scattered"], NBATCH)

            def col_bin(c, f):
                return slots1[:, bass.ds(c, 1), f, :].rearrange("p a c -> p (a c)")

            def bins2_of(c, j):
                v.tensor_tensor(bins2[:, j], iota_2[:, :, :], along(col_bin(c, 0), [P, NB2, SLOTS], 1), ALU.is_equal).then_inc(S["l2_bins"], 1)
                dve.wait_ge(S["l2_bins"], 2 * c + 1)
                v.tensor_tensor_scan(scan2.rearrange("p b c -> p (b c)"), mask_2[:, :, :].rearrange("p b c -> p (b c)"),
                                     bins2[:, j].rearrange("p b c -> p (b c)"), 0.0, ALU.mult, ALU.add).then_inc(S["l2_bins"], 1)

            def spread_of(c, j, h, first):
                w = (j + h) % 2
                if not (first and h < 2):
                    dve.wait_ge(S["l2_scattered"], c * THIRDS + (h - 1))
                s = slice(h * BATCH, (h + 1) * BATCH)
                fields = slots1[:, bass.ds(c, 1), 1:F1, s].rearrange("p a f c -> p (a f) c")
                v.tensor_tensor(spread[:, w].rearrange("p (b f) c -> p b f c", f=F2),
                                along(bins2[:, j, :, s], [P, NB2, F2, BATCH], 2), along(fields, [P, NB2, F2, BATCH], 1), ALU.mult)

            def slots2_of(c, j, h):
                w = (j + h) % 2
                dve.wait_ge(S["l2_rank"], c * THIRDS + (h + 1))
                v.tensor_reduce(rk[:, w, :].rearrange("p (k c) -> p k c", k=2),
                                ps[:, 4:6, 0:NB2 * HALF_BANK].rearrange("p k (b c) -> p k c b", c=HALF_BANK), AX.X, ALU.max).then_inc(S["l2_rank_read"], 1)
                dve.wait_ge(S["l2_rank_read"], c * THIRDS + (h + 1))
                r = rank2[:, bass.ds(c, 1), h * BATCH:(h + 1) * BATCH].rearrange("p a c -> p (a c)")
                v.tensor_scalar(r, rk[:, w, :], -BIG, None, ALU.add).then_inc(S["rank_rounded"], 1)
                dve.wait_ge(S["rank_rounded"], c * THIRDS + (NBATCH + h + 1))
                v.tensor_tensor(onehot_slot[:, w], iota_s[:, :, :], along(r, [P, P, BATCH], 1), ALU.is_equal).then_inc(S["l2_slots"], 1)

            def level3(k, j, g, early):
                a, n = GROUPS[g]
                w = (j + g) % 2
                if g == 0:
                    dve.wait_ge(S["l2_stored"], k + 1)
                if not (early and g < 2):
                    dve.wait_ge(S["l3_built"], k * NG + (g - 1))
                s = slice(a, a + n)
                v.tensor_tensor(onehot_r[:, w, :, 0:n], iota_s[:, 0:RB, 0:n], along(slots2[:, j, 1, s], [P, RB, n], 1), ALU.is_equal).then_inc(S["l3_onehot"], 1)
                v.tensor_tensor(onehot_c[:, w, :, 0:n], iota_s[:, :, 0:n], along(slots2[:, j, 0, s], [P, P, n], 1), ALU.is_equal)
                dve.wait_ge(S["l3_onehot"], k * NG + (g + 1))
                v.tensor_tensor(valued[:, w, :, :, 0:n], along(onehot_r[:, w, :, 0:n], [P, RB, 3, n], 2),
                                along(slots2[:, j, 2:F2, s], [P, RB, 3, n], 1), ALU.mult).then_inc(S["l3_ready"], 1)

            def step(c, j, l2=True, l3=True, first=False, early=False, more=True):
                for h in range(THIRDS):
                    if l2:
                        spread_of(c, j, h, first)
                    if l3:
                        for g in range(h * 2, min(h * 2 + 2, NG) if h < THIRDS - 1 else NG):
                            level3(c - 1, 1 - j, g, early)
                    if l2:
                        slots2_of(c, j, h)
                if l2 and more:
                    bins2_of(c + 1, 1 - j)

            bins2_of(0, 0)
            step(0, 0, l3=False, first=True)
            step(1, 1, early=True)
            with dve.Fori(1, (NB1 - 2) // 2) as pair:
                c = 2 * pair
                step(c, 0)
                step(c + 1, 1)
            step(NB1 - 2, 0)
            step(NB1 - 1, 1, more=False)
            step(NB1, 0, l2=False)

            parts = S["flag_parts"]
            v.tensor_reduce(worst[:, 0:1], rank1[:, :], AX.X, ALU.max)
            v.tensor_reduce(worst[:, 1:2], rank2[:, :, :], AX.XY, ALU.max).then_inc(parts, 1)
            dve.wait_ge(parts, 1)
            v.tensor_tensor(over[:, 0:1], worst[:, 0:1], worst[:, 1:2], ALU.max)
            v.tensor_tensor(over[:, 1:2], worst[:, 2:3], worst[:, 3:4], ALU.max).then_inc(parts, 1)
            dve.wait_ge(parts, 2)
            v.tensor_scalar(over[:, 0:1], over[:, 0:1], P - 0.5, None, ALU.is_gt)
            v.tensor_scalar(over[:, 1:2], over[:, 1:2], GRAPH - 0.5, None, ALU.is_gt).then_inc(parts, 1)
            dve.wait_ge(parts, 3)
            v.tensor_tensor(over[:, 2:3], over[:, 0:1], over[:, 1:2], ALU.add).then_inc(S["flag_vec"], 1)
            dve.wait_ge(S["flag_sum"], 1)
            v.tensor_copy(flag[:, :], ps[0:1, 6, 0:1]).then_inc(S["flag_ready"], 1)
            dve.wait_ge(S["flag_ready"], 1)
            overflow = dve.value_load(flag[0:1, 0:1])

            def fallback(l):
                def stage(t):
                    v.tensor_copy(s_col[:, :], cols_i[:, bass.ds(t, 1)])
                    v.tensor_copy(s_rv[:, :], rv[:, bass.ds(t, 1), :].rearrange("p a b -> p (a b)")).then_inc(S["s_staged"], 1)

                def products(t, first):
                    n = t + (l * ET + 1)
                    dve.wait_ge(S["s_staged"], n)
                    dve.wait_ge(S["s_gathered"], n * 16)
                    v.tensor_scalar(s_gv[:, :], s_g[:, :], s_rv[:, 1:2], None, ALU.mult).then_inc(S["s_scaled"], 1)
                    for b in range(OB):
                        if not (first and b < 2):
                            dve.wait_ge(S["s_summed"], t * OB + (l * ET * OB + b - 1))
                        v.tensor_scalar(lk[:, b % 2, :], s_iota, s_rv[:, 0:1], -float(b * BANK), ALU.subtract, ALU.is_equal).then_inc(S["s_onehot"], 1)
                    dve.wait_ge(S["s_summed"], t * OB + (l * ET * OB + OB))

                dve.wait_ge(S["s_counted"], l + 1)
                stage(0)
                products(0, l == 0)
                with dve.Fori(1, ET) as t:
                    stage(t)
                    products(t, False)
                v.tensor_copy(stack[0:D, 0:N], ps[0:D, :, :].rearrange("p b c -> p (b c)")[:, 0:N]).then_inc(S["s_side"], 1)
                dve.wait_ge(S["s_side"], l + 1)

            for l in range(L):
                dve.wait_ge(S["side_added"], NB1 * (l + 1))
                if l == 0:
                    v.memset(stack[0:D, GRAPH:NCOL], 0.0)
                else:
                    dve.wait_ge(S["e_copied"], NCH)
                for q in range(SQ):
                    v.tensor_copy(stack[0:D, q * CHUNK:(q + 1) * CHUNK], side_piece(q)).then_inc(S["side_ready"], 1)
                dve.wait_ge(S["side_ready"], (l + 1) * SQ)
                with dve.If(overflow):
                    fallback(l)
                ego = emb01 if l == 0 else emb2

                def mult(k):
                    a, w = CH[k]
                    v.tensor_tensor(stack[D:P, a:a + w], ego[0:D, a:a + w], stack[0:D, a:a + w], ALU.mult).then_inc(S["stack_ready"], 1)
                mult(0)
                for k, (a, w) in enumerate(CH):
                    n = l * NCH + k
                    if k + 1 < NCH:
                        mult(k + 1)
                    dve.wait_ge(S["zb_ready"], n + 1)
                    if n >= 2:
                        dve.wait_ge(S["e_ready"], n - 1)
                    v.scalar_tensor_tensor(out=lk[:, k % 2, 0:w], in0=zb[:, k % 2, 0:w], scalar=0.01, in1=zb[:, k % 2, 0:w],
                                           op0=ALU.mult, op1=ALU.max).then_inc(S["lk_ready"], 1)
                    if l == 0:
                        dve.wait_ge(S["e_ready"], n + 1)
                        v.tensor_copy(ego_nm[0:CB, a // CB:(a + w) // CB, :],
                                      ps[0:CB, 3, 0:w // CB * D].rearrange("p (t d) -> p t d", d=D)).then_inc(S["nm2_copied"], 1)

            def row_max(ut):
                dve.wait_ge(S["score_ready"], ut + 1)
                v.tensor_reduce(sc[:, ut, 0:1], ps[:, ut % 2 * Q:ut % 2 * Q + Q, 0:QC], AX.XY, ALU.max).then_inc(S["max_ready"], 1)
                dve.wait_ge(S["max_ready"], 2 * ut + 1)
                v.tensor_scalar(sc[:, ut, 1:2], sc[:, ut, 0:1], -1.0, None, ALU.mult).then_inc(S["max_ready"], 1)

            def subtract(ut):
                dve.wait_ge(S["ln_ready"], ut + 1)
                v.tensor_tensor(sc[:, ut, 4:5], sc[:, ut, 0:1], sc[:, ut, 3:4], ALU.add).then_inc(S["shift_ready"], 1)
                dve.wait_ge(S["shift_ready"], ut + 1)
                if ut >= 2:
                    dve.wait_ge(stored_out[ut % 2], 16 * (ut // 2))
                v.tensor_scalar(res[:, ut % 2, 0:NI].rearrange("p (q c) -> p q c", q=Q), ps[:, ut % 2 * Q:ut % 2 * Q + Q, 0:QC],
                                sc[:, ut, 4:5], None, ALU.subtract).then_inc(S["res_ready"], 1)

            for ut in range(UT):
                row_max(ut)
                if ut:
                    subtract(ut - 1)
            subtract(UT - 1)

        @block.scalar
        def _(act):
            def copy(o, i):
                return nc.scalar.activation(o, i, ACT.Copy)

            act.wait_ge(S["pads_zeroed"], 1)

            def store1(m, j):
                act.wait_ge(S["l1_scattered"], m + 1)
                copy(slots1[:, :, :, bass.ds(m, 1)].rearrange("p b f a -> p (b f a)"), ps[:, 6 + j, 0:NB1 * F1]).then_inc(S["l1_stored"], 1)

            with act.Fori(0, (NBATCH - 1) // 2) as pair:
                m = 2 * pair
                store1(m, 0)
                store1(m + 1, 1)
            store1(NBATCH - 1, 0)

            for g in range(NTG):
                act.wait_ge(S["tr_ready"], g + 1)
                w = min(TG * P, N - g * TG * P)
                copy(emb01[0:D, g * TG * P:g * TG * P + w], ps[0:D, g, 0:w]).then_inc(S["tr_copied"], 1)
            for l in range(L):
                act.wait_ge(S["tr_ready"], NTG + l + 1)
                copy(wT[:, l, :], ps[:, l, 0:P]).then_inc(S["tr_copied"], 1)
            for g in range(NMG):
                act.wait_ge(S["nm_ready"], g + 1)
                n = min(GW, NT - g * GW)
                copy(ego_nm[0:CB, g * GW:g * GW + n, :], ps[0:CB, g, 0:n * D].rearrange("p (t d) -> p t d", d=D)).then_inc(S["nm_copied"], 1)

            def store3(k, j, g, early):
                a, n = GROUPS[g]
                act.wait_ge(S["l3_built"], k * NG + (g + 1))
                if g == 0 and not early:
                    act.wait_ge(S["side_added"], k - 1)
                    act.wait_ge(block_saved[j], (k - j) * 8)
                copy(work[:, j, a * RB:(a + n) * RB], ps[:, 6 + (j + g) % 2, 0:n * RB]).then_inc(S["l3_stored"], 1)

            def store2(c, j, early):
                act.wait_ge(S["l2_scattered"], c * THIRDS + THIRDS)
                if not early:
                    act.wait_ge(S["l3_ready"], (c - 1) * NG)
                copy(slots2[:, j], ps[:, 3, 0:NB2 * F2].rearrange("p (b f) -> p f b", f=F2)).then_inc(S["l2_stored"], 1)

            def step(c, j, l2=True, l3=True, early3=False, early2=False):
                if l3:
                    for g in range(NG):
                        store3(c - 1, 1 - j, g, early3)
                if l2:
                    store2(c, j, early2)

            step(0, 0, l3=False, early2=True)
            step(1, 1, early3=True, early2=True)
            step(2, 0, early3=True)
            step(3, 1)
            with act.Fori(2, (NB1) // 2) as pair:
                c = 2 * pair
                step(c, 0)
                step(c + 1, 1)
            step(NB1, 0, l2=False)

            for l in range(L):
                def add_bias(k):
                    n = l * NCH + k
                    w = CH[k][1]
                    act.wait_ge(S["z_ready"], n + 1)
                    if n >= 2:
                        act.wait_ge(S["lk_ready"], n - 1)
                    nc.scalar.activation(zb[:, k % 2, 0:w], ps[:, 4 + k % 2, 0:w], ACT.Identity, bias=bias[:, l:l + 1]).then_inc(S["zb_ready"], 1)

                add_bias(0)
                for k, (a, w) in enumerate(CH):
                    act.wait_ge(S["e_ready"], l * NCH + k + 1)
                    if l == 0:
                        copy(emb01[D:P, a:a + w], ps[0:D, 6 + k % 2, 0:w])
                    copy(emb2[0:D, a:a + w], ps[0:D, 6 + k % 2, 0:w]).then_inc(S["e_copied"], 1)
                    if k + 1 < NCH:
                        add_bias(k + 1)
            for ut in range(UT):
                act.wait_ge(S["max_ready"], 2 * ut + 2)
                if ut:
                    act.wait_ge(S["exp_ready"], ut)
                nc.scalar.activation(junk.rearrange("p (q c) -> p q c", q=Q), ps[:, ut % 2 * Q:ut % 2 * Q + Q, 0:QC], ACT.Exp,
                                     bias=sc[:, ut, 1:2], accum_out=sc[:, ut, 2:3]).then_inc(S["exp_ready"], 1)
                act.wait_ge(S["exp_ready"], ut + 1)
                nc.scalar.activation(sc[:, ut, 3:4], sc[:, ut, 2:3], ACT.Ln).then_inc(S["ln_ready"], 1)


_INS = ["r_user_indices", "L0_rec_item_indices", "L0_rec_adj_rows", "L0_rec_adj_cols", "L0_rec_adj_vals",
        "L0_rec_user_emb", "L0_rec_item_emb", "L0_rec_gc_W", "L0_rec_gc_b", "L0_rec_bi_W", "L0_rec_bi_b"]


def kernel(**inputs):
    import numpy as np
    import concourse.bacc as bacc
    from concourse.bass_utils import run_bass_kernel_spmd

    nc = bacc.Bacc("TRN2", target_bir_lowering=False, num_devices=1)
    arrays, args = {}, []
    for name in _INS:
        a = np.ascontiguousarray(inputs[name])
        arrays[f"in_{name}"] = a
        args.append(nc.dram_tensor(f"in_{name}", a.shape, mybir.dt.from_np(a.dtype), kind="ExternalInput").ap())
    shape = (inputs["r_user_indices"].shape[0], inputs["L0_rec_item_indices"].shape[0])
    args.append(nc.dram_tensor("out_scores", shape, F32, kind="ExternalOutput").ap())
    build(nc, *args)
    r = run_bass_kernel_spmd(nc, [arrays], core_ids=[0])
    return r.results[0]["out_scores"]
```

```python
from contextlib import ExitStack

import concourse.bass as bass
from concourse import mybir

ALU = mybir.AluOpType
ACT = mybir.ActivationFunctionType
AX = mybir.AxisListType
F32 = mybir.dt.float32
BF16 = mybir.dt.bfloat16
I32 = mybir.dt.int32
U32 = mybir.dt.uint32
I16 = mybir.dt.int16

P = 128
BANK = 512
BATCH = 16
ROUND = 12582912.0
BIG = 8193.0
CB = 125
RB = 60
CHUNK = 500


def build(nc, user_idx, item_idx, adj_rows, adj_cols, adj_vals, user_emb, item_emb,
          gc_W, gc_b, bi_W, bi_b, out):
    NU, NI = user_idx.shape[0], item_idx.shape[0]
    D = user_emb.shape[1]
    L = gc_W.shape[0]
    N = NU + NI
    GRAPH = user_emb.shape[0] + item_emb.shape[0]
    UT = NU // P
    IT = -(-NI // P)
    GT = UT + IT
    LAST = NI - (IT - 1) * P
    NT = -(-N // CB)
    NCOL = NT * CB
    ET = adj_rows.shape[0] // P
    NB1 = GRAPH // CB
    NB2 = GRAPH // RB
    NBATCH = -(-ET // BATCH)
    EP = NBATCH * BATCH
    THIRDS = -(-NBATCH // BATCH)
    SLOTS = THIRDS * BATCH
    GW = 8
    NG = -(-NB2 // GW)
    TB = 2 * GW
    GROUPS = [(a, min(GW, NB2 - a)) for a in range(0, NB2, GW)]
    THIRD_OF = [min(g // 2, THIRDS - 1) for g in range(NG)]
    SPAN = [(TB * h, (TB if h < THIRDS - 1 else NB2 - TB * h)) for h in range(THIRDS)]
    PAIRS3 = (NB2 - TB * (THIRDS - 1)) // 2
    F1 = 5
    F2 = F1 - 1
    PLACE = 64
    SQ = GRAPH // CHUNK
    UNITS = SLOTS // GW
    LATE = 4
    HELD = 4
    SPILLED = NB1 - 2 - HELD
    CH = [(a, min(CHUNK, NCOL - a)) for a in range(0, NCOL, CHUNK)]
    NCH = len(CH)
    Q = 4
    QC = NI // Q
    HQ = Q // 2
    TG = 4
    NTG = GT // TG
    NMG = -(-NT // GW)
    NPIECE = NTG + L + NMG
    STOPS = [8 + 2 * i for i in range(-(-NPIECE // 2))]
    OB = 8
    FULL = -(-NB1 * CB // CHUNK) - 1
    assert 2 * D == P and L == 2 and GRAPH == NB1 * CB == NB2 * RB and N <= OB * BANK
    assert NBATCH % 2 == 1 and NB1 % 2 == 0 and SLOTS > NBATCH and SPILLED % 2 == 0

    with ExitStack() as ctx:
        def sb(name, shape, dt=F32):
            return ctx.enter_context(nc.sbuf_tensor(name, shape, dt))

        def sem(name):
            return ctx.enter_context(nc.semaphore(name))

        class Arena:

            def __init__(self, name, words):
                self.mem, self.at, self.words = sb(name, [P, words]), 0, words

            def take(self, shape, dt=F32):
                n = 1
                for s in shape:
                    n *= s
                w = n if dt in (F32, I32) else -(-n // 2)
                v = self.mem[:, self.at:self.at + w]
                self.at += w
                assert self.at <= self.words, (self.at, self.words)
                if dt != F32:
                    v = v.bitcast(dt)[:, 0:n]
                names = "abcdefg"[:len(shape)]
                if len(shape) > 1:
                    v = v.rearrange(f"p ({' '.join(names)}) -> p {' '.join(names)}", **dict(zip(names, shape)))
                return v

            def reuse(self):
                self.at = 0

        ps = ctx.enter_context(nc.psum_tensor("ps", [P, 8, BANK], F32))
        spill = nc.dram_tensor("spilled_blocks", [SPILLED, P, GRAPH], F32, kind="Internal").ap()
        table = nc.dram_tensor("ego_table", [NCOL, D], F32, kind="Internal").ap()

        idx = sb("idx", [P, GT], I32)
        ident = sb("ident", [P, P])
        fold = sb("fold", [P, D])
        wblk = sb("wblk", [P, L, P])
        wT = sb("wT", [P, L, P])
        bias = sb("bias", [P, L])
        emb01 = sb("emb01", [P, NCOL])
        ego_nm = sb("ego_nm", [P, NT, D])
        zeros = sb("zeros", [P, BANK], BF16)
        iota_s = sb("iota_s", [P, P + 1, 2], I16)
        iota_1 = sb("iota_1", [P, P, 2], I16)
        iota_b = sb("iota_b", [P, NB2 + 1, 2], BF16)
        tile_count1 = sb("tile_count1", [P, 2, NB1], BF16)
        earlier = sb("earlier", [P, P], BF16)
        before = sb("before", [P, SLOTS], BF16)
        select = sb("select", [P, 2 * SLOTS - 1], BF16)
        tile_count = sb("tile_count", [P, NB2], BF16)
        rows_i = sb("rows_i", [P, ET], I32)
        cols_i = sb("cols_i", [P, ET], I32)
        vals = sb("vals", [P, ET])
        rank1 = sb("rank1", [P, EP], I16)
        rank2 = sb("rank2", [P, NB1, SLOTS], I16)
        rk = sb("rk", [P, 2, BATCH])
        lhs = sb("lhs", [P, 2, D])
        worst = sb("worst", [P, 4])
        over = sb("over", [P, 3])
        flag = sb("flag", [1, 1], I32)
        one_f = sb("one_f", [P, 1])
        below = sb("below", [P, 1])
        work = sb("work", [P, 2, GRAPH])
        s_col = sb("s_col", [P, 1], I32)
        s_idx = sb("s_idx", [P, 1], I32)
        s_zero = sb("s_zero", [P, 1], I32)
        s_rv = sb("s_rv", [P, 2])
        s_g = sb("s_g", [P, D])
        s_gv = sb("s_gv", [P, D])
        sc = sb("sc", [P, UT, 7])

        held_mem = Arena("held_mem", HELD * GRAPH)
        held = held_mem.take([HELD, GRAPH])
        held_mem.reuse()
        gath = held_mem.take([GT, D])
        col_bin_f, col_in_bin, row_bin_f, row_in_bin, rest = (held_mem.take([ET]) for _ in range(5))
        cbin = held_mem.take([EP], BF16)
        pay = held_mem.take([F1, EP], BF16)

        HB = BATCH // 2
        work_mem = Arena("work_mem", 2 * NCOL + LATE * GRAPH)
        slots1 = work_mem.take([NB1, F1, SLOTS], BF16)
        onehot_slot = work_mem.take([2, HB, P, 2], BF16)
        spread2 = work_mem.take([3, NB2 * F2, BATCH], BF16)
        spread1 = spread2[:, :, 0:NB1 * F1, :]
        bins2 = work_mem.take([2, NB2, SLOTS], BF16)
        slots2 = work_mem.take([2, F2, NB2], BF16)
        place_c = work_mem.take([NB2], I16)
        place_r = work_mem.take([NB2], I16)
        onehot_c = work_mem.take([2, PAIRS3, P, 2], BF16)
        onehot_r = work_mem.take([RB, 2 * PAIRS3], BF16)
        valued = work_mem.take([2, RB, 3, 2 * PAIRS3], BF16)
        matched = work_mem.take([2, BATCH, NB2], BF16)
        bins1 = bins2.rearrange("p a b c -> p (a b c)")[:, 0:2 * NB1 * BATCH].rearrange("p (a b c) -> p a b c", a=2, b=NB1)
        work_mem.reuse()
        stack = work_mem.take([NCOL])
        emb2 = work_mem.take([NCOL])
        late = work_mem.take([LATE, GRAPH])
        zb = sb("zb", [P, 2, CHUNK])
        lk = sb("lk", [P, 2, BANK])
        s_iota = zb[:, :, :].rearrange("p a b -> p (a b)")[:, 0:BANK]
        res = work
        junk = held_mem.mem[:, 0:NI // 2].bitcast(BF16)

        names = """idx_loaded w_loaded cols_loaded rows_loaded vals_loaded consts_ready zeroed gathered
            prep_done value_parts
            l1_bins l1_counted l1_count_read l1_spread rank_rounded l1_rank l1_rank_read l1_slots l1_scattered l1_stored
            tr_ready tr_copied nm_ready nm_copied pads_zeroed
            l2_bins l2_counted l2_count_read l2_rank l2_rank_read l2_slots l2_scattered l2_stored
            l3_places l3_onehot l3_ready l3_built l3_stored lhs_ready side_added
            flag_parts flag_vec flag_sum flag_ready table_written
            s_counted s_staged s_gathered s_scaled s_onehot s_summed s_side
            side_ready stack_ready z_ready zb_ready lk_ready e_ready e_copied emb1_copied
            nm2_ready nm2_copied score_ready max_parts max_ready exp_ready ln_ready shift_ready
            left_ready right_ready""".split()
        S = {n: sem(n) for n in names}
        stored_out = [sem("stored_out0"), sem("stored_out1")]
        block_saved = [sem("block_saved0"), sem("block_saved1")]
        NSLOT = 2 + HELD + LATE
        block_back = [sem(f"block_back{i}") for i in range(NSLOT)]

        ORDER = [NB1 - 2, NB1 - 1] + list(range(SPILLED, NB1 - 2)) + list(range(SPILLED))
        NRES = 2 + HELD

        def ring(i):
            s = i % NSLOT
            if s < 2:
                return work[:, s, :]
            if s < NRES:
                return held[:, s - 2, :]
            return late[:, s - NRES, :]

        def side_piece(q):
            return ps[(q % 2) * D:(q % 2) * D + D, q // 2, 0:CHUNK]

        def group_bank(g):
            return (g + (g >= 4)) % 2

        def node_bank(k):
            return 2 + k % 2 if k <= FULL else 3

        def at(x):
            return bass.ds(x, 1)

        block = ctx.enter_context(nc.Block())

        @block.sync
        def _(sp):
            with nc.allow_non_contiguous_dma("small loads across partitions"):
                sp.dma_start(cols_i[:, :], adj_cols.rearrange("(p t) -> p t", p=P)).then_inc(S["cols_loaded"], 16)
                sp.dma_start(rows_i[:, :], adj_rows.rearrange("(p t) -> p t", p=P)).then_inc(S["rows_loaded"], 16)
                sp.dma_start(vals[:, :], adj_vals.rearrange("(p t) -> p t", p=P)).then_inc(S["vals_loaded"], 16)
                sp.dma_start(idx[:, 0:UT], user_idx.rearrange("(t p) -> p t", p=P)).then_inc(S["idx_loaded"], 16)
                sp.dma_start(idx[:, UT:GT - 1], item_idx[0:(IT - 1) * P].rearrange("(t p) -> p t", p=P)).then_inc(S["idx_loaded"], 16)
                sp.dma_start(idx[0:LAST, GT - 1:GT], item_idx[(IT - 1) * P:NI].rearrange("(p a) -> p a", a=1)).then_inc(S["idx_loaded"], 16)
                sp.wait_ge(S["zeroed"], 1)
                for l in range(L):
                    sp.dma_start(wblk[0:D, l, 0:D], gc_W[l]).then_inc(S["w_loaded"], 16)
                    sp.dma_start(wblk[D:P, l, D:P], bi_W[l]).then_inc(S["w_loaded"], 16)
                    sp.dma_start(bias[0:D, l:l + 1], gc_b[l].rearrange("(p a) -> p a", a=1)).then_inc(S["w_loaded"], 16)
                    sp.dma_start(bias[D:P, l:l + 1], bi_b[l].rearrange("(p a) -> p a", a=1)).then_inc(S["w_loaded"], 16)

            with sp.Fori(0, (SPILLED) // 2) as pair:
                k = 2 * pair
                for j in range(2):
                    sp.wait_ge(S["l3_stored"], k * NG + NG * (j + 1))
                    sp.dma_start(spill[at(k + j), :, :].rearrange("a p c -> p (a c)"), work[:, j, :]).then_inc(block_saved[j], 16)
            for k in range(SPILLED, NB1 - 2):
                sp.wait_ge(S["l3_stored"], NG * (k + 1))
                sp.dma_start(held[:, k - SPILLED, :], work[:, k % 2, :]).then_inc(block_saved[k % 2], 16)

            def bring_back(i):
                if i >= NRES and i < NSLOT:
                    sp.wait_ge(S["l3_built"], NB1 * NG)
                if i >= NSLOT:
                    sp.wait_ge(S["side_added"], NB1 + 1 + i - NSLOT)
                sp.dma_start(ring(i), spill[ORDER[i]]).then_inc(block_back[i % NSLOT], 16)

            for j in range(2):
                sp.wait_ge(block_saved[j], 16 * (NB1 // 2 - 1))
            for i in range(NRES, NSLOT):
                bring_back(i)

            def fallback(l):
                sp.wait_ge(S["nm_copied"], NMG)
                if l:
                    sp.wait_ge(S["nm2_copied"], NCH)
                sp.dma_start(table.rearrange("(t p) d -> p t d", p=CB), ego_nm[0:CB, :, :]).then_inc(S["table_written"], 16)

            sp.wait_ge(S["flag_ready"], 1)
            overflow = sp.value_load(flag[0:1, 0:1])
            with sp.If(overflow):
                fallback(0)
            for i in range(NSLOT, NB1):
                bring_back(i)
            with sp.If(overflow):
                fallback(1)
            for ut in range(UT):
                for side, a in (("left_ready", 0), ("right_ready", HQ * QC)):
                    sp.wait_ge(S[side], ut + 1)
                    sp.dma_start(out[ut * P:(ut + 1) * P, a:a + HQ * QC], res[:, ut % 2, a:a + HQ * QC]).then_inc(stored_out[ut % 2], 16)
            for s in range(2):
                sp.wait_ge(stored_out[s], 32 * (UT // 2))

        @block.gpsimd
        def _(pool):
            ready = S["consts_ready"]
            nc.gpsimd.memset(earlier[:, :], 1.0)
            nc.gpsimd.memset(before[:, :], 1.0)
            nc.gpsimd.memset(select[:, :], 0.0)
            nc.gpsimd.memset(ident[:, :], 0.0)
            nc.gpsimd.memset(fold[:, :], 0.0)
            nc.gpsimd.memset(s_zero[:, :], 0)
            nc.gpsimd.memset(zeros[:, :], 0.0)
            nc.gpsimd.memset(one_f[:, :], 1.0)
            nc.gpsimd.memset(below[:, :], 2.0 - BIG)
            nc.gpsimd.memset(wblk[:, :, :], 0.0).then_inc(S["zeroed"], 1)
            pool.wait_ge(S["zeroed"], 1)
            nc.gpsimd.memset(select[:, SLOTS - 1:SLOTS], 1.0)
            nc.gpsimd.affine_select(out=earlier[:, :], in_=earlier[:, :], compare_op=ALU.is_gt, fill=0.0,
                                    base=0, pattern=[[1, P]], channel_multiplier=-1)
            nc.gpsimd.affine_select(out=before[:, :], in_=before[:, :], compare_op=ALU.is_gt, fill=0.0,
                                    base=0, pattern=[[1, SLOTS]], channel_multiplier=-1)
            nc.gpsimd.iota(iota_b[:, :, :], pattern=[[1, NB2 + 1], [0, 2]], base=0, channel_multiplier=0,
                           allow_small_or_imprecise_dtypes=True)
            nc.gpsimd.iota(iota_1[:, :, :], pattern=[[1, P], [0, 2]], base=int(BIG) - 1, channel_multiplier=0,
                           allow_small_or_imprecise_dtypes=True).then_inc(ready, 1)
            pool.wait_ge(ready, 1)
            nc.gpsimd.affine_select(out=earlier[:, :], in_=earlier[:, :], compare_op=ALU.not_equal, fill=BIG - 1,
                                    base=0, pattern=[[-1, P]], channel_multiplier=1).then_inc(ready, 1)
            nc.gpsimd.iota(iota_s[:, :, :], pattern=[[1, P + 1], [0, 2]], base=0, channel_multiplier=0,
                           allow_small_or_imprecise_dtypes=True)
            nc.gpsimd.affine_select(out=ident[:, :], in_=ident[:, :], compare_op=ALU.not_equal, fill=1.0,
                                    base=0, pattern=[[-1, P]], channel_multiplier=1)
            nc.gpsimd.affine_select(out=fold[:, :], in_=fold[:, :], compare_op=ALU.not_equal, fill=1.0,
                                    base=0, pattern=[[-1, D]], channel_multiplier=1).then_inc(ready, 1)
            pool.wait_ge(ready, 3)
            nc.gpsimd.affine_select(out=fold[:, :], in_=fold[:, :], compare_op=ALU.not_equal, fill=1.0,
                                    base=-D, pattern=[[-1, D]], channel_multiplier=1).then_inc(ready, 1)
            pool.wait_ge(S["idx_loaded"], 48)
            for t in range(GT):
                n = LAST if t == GT - 1 else P
                src = user_emb if t < UT else item_emb
                nc.gpsimd.indirect_dma_start(
                    gath[0:n, t, :], None, src,
                    bass.IndirectOffsetOnAxis(ap=idx[0:n, t:t + 1].bitcast(U32), axis=0)).then_inc(S["gathered"], 16)

            def hand_over(k, j):
                nc.gpsimd.tensor_copy(lhs[0:CB, j, :], ego_nm[0:CB, at(k), :].rearrange("p a d -> p (a d)")).then_inc(S["lhs_ready"], 1)
            pool.wait_ge(S["nm_copied"], NMG)
            hand_over(0, 0)
            hand_over(1, 1)
            with pool.Fori(1, (NB1) // 2) as pair:
                k = 2 * pair
                for j in range(2):
                    pool.wait_ge(S["side_added"], k + (j - 1))
                    hand_over(k + j, j)

            def fallback(l):
                if l:
                    pool.wait_ge(S["lk_ready"], l * NCH)
                nc.gpsimd.iota(s_iota, pattern=[[1, BANK]], base=0, channel_multiplier=0,
                               allow_small_or_imprecise_dtypes=True).then_inc(S["s_counted"], 1)
                pool.wait_ge(S["table_written"], 16 * (l + 1))
                with pool.Fori(0, ET) as t:
                    pool.wait_ge(S["s_staged"], t + (l * ET + 1))
                    nc.gpsimd.tensor_tensor(s_idx[:, :], s_col[:, :], s_zero[:, :], ALU.add)
                    nc.gpsimd.drain()
                    nc.gpsimd.indirect_dma_start(
                        s_g[:, :], None, table,
                        bass.IndirectOffsetOnAxis(ap=s_idx[:, :].bitcast(U32), axis=0)).then_inc(S["s_gathered"], 16)

            pool.wait_ge(S["flag_ready"], 1)
            overflow = pool.value_load(flag[0:1, 0:1])
            with pool.If(overflow):
                fallback(0)
                fallback(1)

        @block.tensor
        def _(pe):
            mm = nc.tensor.matmul

            def count1_of(m, j, first=False):
                pe.wait_ge(S["l1_bins"], m + 1)
                if not first:
                    pe.wait_ge(S["l1_count_read"], m - 1)
                for t in range(BATCH):
                    x = mm(ps[0:BATCH, j, 0:NB1], select[:, SLOTS - 1 - t:SLOTS - 1 - t + BATCH], bins1[:, j, :, t],
                           start=(t == 0), stop=(t == BATCH - 1))
                x.then_inc(S["l1_counted"], 1)

            def rank1_of(m, j, first=False):
                pe.wait_ge(S["l1_count_read"], m + 1)
                if not first:
                    pe.wait_ge(S["l1_rank_read"], m - 1)
                o = ps[:, 4 + j, 0:NB1 * BATCH].rearrange("p (b c) -> p b c", b=NB1)
                mm(o, earlier[:, :], bins1[:, j], start=True, stop=True)
                for t in range(BATCH):
                    x = mm(o[:, :, t], before[0:BATCH, t:t + 1].to_broadcast([BATCH, P]), tile_count1[0:BATCH, j, :],
                           start=False, stop=True, skip_group_check=True)
                x.then_inc(S["l1_rank"], 1)

            def scatter1(m, j, first=False):
                pe.wait_ge(S["l1_slots"], m + 1)
                if not first:
                    pe.wait_ge(S["l1_stored"], m - 1)
                for t in range(BATCH):
                    x = mm(ps[:, 6 + j, 0:NB1 * F1], onehot_slot[:, j, t // 2, :, t % 2], spread1[:, j, :, t], start=(t == 0), stop=(t == BATCH - 1))
                x.then_inc(S["l1_scattered"], 1)

            def batch_step(m, j, first=False, last=False):
                if not last:
                    count1_of(m + 1, 1 - j, isinstance(m, int) and m < 1)
                if not (isinstance(m, int) and m < 1):
                    scatter1(m - 1, 1 - j, first)
                if not last:
                    rank1_of(m + 1, 1 - j, isinstance(m, int) and m < 1)

            pe.wait_ge(S["consts_ready"], 2)
            count1_of(0, 0, True)
            rank1_of(0, 0, True)
            batch_step(0, 0)
            batch_step(1, 1, first=True)
            batch_step(2, 0, first=True)
            batch_step(3, 1)

            def piece(i):
                o = 2 + i % 2
                if i < NTG:
                    if i == 0:
                        pe.wait_ge(S["consts_ready"], 4)
                        pe.wait_ge(S["gathered"], 16 * GT)
                    if i >= 2:
                        pe.wait_ge(S["tr_copied"], i - 1)
                    for k in range(TG):
                        t = i * TG + k
                        n = LAST if t == GT - 1 else P
                        x = nc.tensor.transpose(ps[0:D, o, k * P:k * P + n], gath[0:n, t, :], ident[0:n, 0:n])
                    x.then_inc(S["tr_ready"], 1)
                elif i < NTG + L:
                    if i == NTG:
                        pe.wait_ge(S["w_loaded"], 16 * 4 * L)
                    pe.wait_ge(S["tr_copied"], i - 1)
                    nc.tensor.transpose(ps[:, o, 0:P], wblk[:, i - NTG, :], ident[:, :]).then_inc(S["tr_ready"], 1)
                else:
                    g = i - NTG - L
                    if g == 0:
                        pe.wait_ge(S["tr_copied"], NTG + L)
                    if g >= 2:
                        pe.wait_ge(S["nm_copied"], g - 1)
                    for k in range(min(GW, NT - g * GW)):
                        a = (g * GW + k) * CB
                        x = nc.tensor.transpose(ps[0:CB, o, k * D:(k + 1) * D], emb01[0:D, a:a + CB], ident[0:D, 0:D])
                    x.then_inc(S["nm_ready"], 1)

            at_pair = 2
            for n, stop in enumerate(STOPS + [(NBATCH - 1) // 2]):
                with pe.Fori(at_pair, stop) as pair:
                    m = 2 * pair
                    batch_step(m, 0)
                    batch_step(m + 1, 1)
                at_pair = stop
                for i in range(2 * n, min(2 * n + 2, NPIECE)):
                    piece(i)
            batch_step(NBATCH - 1, 0, last=True)
            scatter1(NBATCH - 1, 0)

            def count2_of(c, j, first=False):
                pe.wait_ge(S["l2_bins"], c + 1)
                if not first:
                    pe.wait_ge(S["l2_count_read"], c)
                    if not isinstance(c, int) or c >= 2:
                        pe.wait_ge(S["l3_stored"], (c - 2) * NG + 3)
                for t in range(SLOTS):
                    x = mm(ps[0:SLOTS, 6, 0:NB2], select[:, SLOTS - 1 - t:2 * SLOTS - 1 - t], bins2[:, j, :, t],
                           start=(t == 0), stop=(t == SLOTS - 1))
                x.then_inc(S["l2_counted"], 1)

            def rank2_of(c, j, u, first=False):
                if u == 0:
                    pe.wait_ge(S["l2_count_read"], c + 1)
                if not (first and u < 2):
                    pe.wait_ge(S["l2_rank_read"], c * UNITS + (u - 1))
                o = ps[:, 4 + u % 2, 0:NB2 * GW].rearrange("p (b c) -> p b c", b=NB2)
                mm(o, earlier[:, :], bins2[:, j, :, u * GW:(u + 1) * GW], start=True, stop=True)
                for i in range(GW):
                    t = u * GW + i
                    x = mm(o[:, :, i], before[0:SLOTS, t:t + 1].to_broadcast([SLOTS, P]), tile_count[0:SLOTS, :],
                           start=False, stop=True, skip_group_check=True)
                x.then_inc(S["l2_rank"], 1)

            def scatter2(c, j, h, first=False):
                pe.wait_ge(S["l2_slots"], THIRDS * c + (h + 1))
                if h == 0 and not first:
                    pe.wait_ge(S["l2_stored"], c)
                w = (j + h) % 2
                for t in range(BATCH):
                    x = mm(ps[:, 3, 0:NB2 * F2], onehot_slot[:, w, t // 2, :, t % 2], spread2[:, h, :, t],
                           start=(h == 0 and t == 0), stop=(h == THIRDS - 1 and t == BATCH - 1))
                x.then_inc(S["l2_scattered"], 1)

            def level3(k, j, g, early, more):
                a, n = GROUPS[g]
                w = group_bank(g)
                h = THIRD_OF[g]
                u = (j + h) % 2
                pe.wait_ge(S["l3_ready"], k * THIRDS + (h + 1))
                if not (early and g < 2):
                    pe.wait_ge(S["l3_stored"], k * NG + (g if g == 4 else g - 1))
                if g == 5 and more:
                    pe.wait_ge(S["l2_count_read"], k + 3)
                for b in range(n):
                    i = a + b - SPAN[h][0]
                    for v in range(3):
                        x = mm(ps[:, 6 + w, b * RB:(b + 1) * RB], onehot_c[:, u, i // 2, :, i % 2], valued[:, u, :, v, i],
                               start=(v == 0), stop=(v == 2))
                x.then_inc(S["l3_built"], 1)

            def add_side(k, j, pieces=range(SQ), groups=NG):
                pe.wait_ge(S["l3_stored"], k * NG + groups)
                pe.wait_ge(S["lhs_ready"], k + 1)
                for q in pieces:
                    x = mm(side_piece(q), lhs[0:CB, j, :], work[0:CB, j, q * CHUNK:(q + 1) * CHUNK],
                           start=False, stop=True, skip_group_check=True)
                if SQ - 1 in pieces:
                    x.then_inc(S["side_added"], 1)

            def step(c, j, l2=True, l3=True, add=True, first=False, more=True, halfway=None):
                def scatter(h):
                    if l2:
                        scatter2(c, j, h, first)

                def ranks(u):
                    if l2:
                        rank2_of(c, j, u, first)

                def groups(*which):
                    for g in which if l3 else ():
                        level3(c - 1, 1 - j, g, isinstance(c, int) and c == 1, l2 and more)

                if add:
                    add_side(c - 2, j)
                ranks(2)
                ranks(3)
                groups(0, 1)
                scatter(0)
                ranks(4)
                ranks(5)
                groups(2, 3)
                if halfway:
                    halfway()
                scatter(1)
                if l2 and more:
                    count2_of(c + 1, 1 - j)
                groups(4)
                if l2 and more:
                    rank2_of(c + 1, 1 - j, 0)
                    rank2_of(c + 1, 1 - j, 1)
                scatter(2)
                groups(5, 6)

            pe.wait_ge(S["l1_stored"], NBATCH)
            pe.wait_ge(S["l1_rank_read"], NBATCH)
            count2_of(0, 0, first=True)
            rank2_of(0, 0, 0, first=True)
            rank2_of(0, 0, 1, first=True)
            pe.wait_ge(S["nm_copied"], NMG)
            for q in range(SQ):
                mm(side_piece(q), zeros[:, 0:D], zeros[:, 0:CHUNK], start=True, stop=True)
            step(0, 0, l3=False, add=False, first=True)
            step(1, 1, add=False)
            with pe.Fori(1, (NB1 - 2) // 2) as pair:
                c = 2 * pair
                step(c, 0)
                step(c + 1, 1)
            step(NB1 - 2, 0)
            step(NB1 - 1, 1, more=False)
            assert SQ // 2 * CHUNK <= 4 * GW * RB
            step(NB1, 0, l2=False, halfway=lambda: add_side(NB1 - 1, 1, range(SQ // 2), 4))
            pe.wait_ge(S["flag_vec"], 1)
            pe.wait_ge(S["l2_rank_read"], NB1 * UNITS)
            mm(ps[0:1, 4, 0:1], over[:, 2:3], one_f[:, :], start=True, stop=True).then_inc(S["flag_sum"], 1)
            add_side(NB1 - 1, 1, range(SQ // 2, SQ))
            pe.wait_ge(S["flag_ready"], 1)
            overflow = pe.value_load(flag[0:1, 0:1])

            def fallback(l):
                pe.wait_ge(S["side_ready"], (l + 1) * SQ)

                def add_tile(t, first):
                    for b in range(OB):
                        pe.wait_ge(S["s_onehot"], t * OB + (l * ET * OB + b + 1))
                        if b == 0:
                            pe.wait_ge(S["s_scaled"], t + (l * ET + 1))
                        mm(ps[0:D, b, :], s_gv[:, :], lk[:, b % 2, :], start=first, stop=True,
                           skip_group_check=True).then_inc(S["s_summed"], 1)
                add_tile(0, True)
                with pe.Fori(1, ET) as t:
                    add_tile(t, False)
                pe.wait_ge(S["s_side"], l + 1)

            def layer2_product(i):
                if i == 0:
                    pe.wait_ge(S["side_ready"], SQ)
                    pe.wait_ge(S["nm2_copied"], FULL + 1)
                    for j in range(2):
                        pe.wait_ge(block_saved[j], 16 * (NB1 // 2 - 1))
                    for q in range(SQ):
                        mm(side_piece(q), zeros[:, 0:D], zeros[:, 0:CHUNK], start=True, stop=True)
                if i >= NRES:
                    pe.wait_ge(block_back[i % NSLOT], 16 * (i // NSLOT + (i % NSLOT >= NRES)))
                for q in range(SQ):
                    x = mm(side_piece(q), ego_nm[0:CB, ORDER[i], :], ring(i)[0:CB, q * CHUNK:(q + 1) * CHUNK],
                           start=False, stop=True, skip_group_check=True)
                x.then_inc(S["side_added"], 1)

            for l in range(L):
                if l:
                    pe.wait_ge(S["nm2_copied"], NCH)
                    for i in range(NCH - FULL, NB1):
                        layer2_product(i)
                with pe.If(overflow):
                    fallback(l)

                def z_of(k):
                    a, w = CH[k]
                    n = l * NCH + k
                    pe.wait_ge(S["stack_ready"], n + 1)
                    if n >= 2:
                        pe.wait_ge(S["zb_ready"], n - 1)
                    mm(ps[:, 4 + k % 2, 0:w], wT[:, l, :], stack[:, a:a + w], start=True, stop=True).then_inc(S["z_ready"], 1)

                pe.wait_ge(S["side_ready"], (l + 1) * SQ)
                z_of(0)
                z_of(1)
                for k, (a, w) in enumerate(CH):
                    n = l * NCH + k
                    pe.wait_ge(S["lk_ready"], n + 1)
                    if n >= 2:
                        pe.wait_ge(S["e_copied"], n - 1)
                    hw = (w + 1) // 2
                    mm(ps[0:D, 6 + k % 2, 0:hw], fold[:, :], lk[:, k % 2, 0:hw], start=True, stop=True)
                    mm(ps[D:P, 6 + k % 2, 0:w - hw], fold[:, :], lk[:, k % 2, hw:w], start=True, stop=True).then_inc(S["e_ready"], 1)
                    if l == 0:
                        if k >= 2:
                            pe.wait_ge(S["nm2_copied"], k if k > FULL else k - 1)
                        for i in range(w // CB):
                            x = mm(ps[0:CB, node_bank(k), i * D:(i + 1) * D], lk[:, k % 2, i * CB:(i + 1) * CB], fold[:, :], start=True, stop=True)
                        x.then_inc(S["nm2_ready"], 1)
                    if k + 2 < NCH:
                        z_of(k + 2)
                    if l == 0 and k >= FULL:
                        layer2_product(k - FULL)

            pe.wait_ge(S["e_copied"], L * NCH)
            for ut in range(UT):
                for q in range(Q):
                    if ut >= 2 and q % HQ == 0:
                        pe.wait_ge(S[("left_ready", "right_ready")[q // HQ]], ut - 1)
                    o = ps[:, (ut % 2) * Q + q, 0:QC]
                    u = slice(ut * P, (ut + 1) * P)
                    i = slice(NU + q * QC, NU + (q + 1) * QC)
                    mm(o, emb01[:, u], emb01[:, i], start=True, stop=False)
                    x = mm(o, emb2[0:D, u], emb2[0:D, i], start=False, stop=True)
                    if q % HQ == HQ - 1:
                        x.then_inc(S["score_ready"], 1)

        @block.vector
        def _(dve):
            v = nc.vector
            done = [0]

            def chain(ins):
                done[0] += 1
                ins.then_inc(S["prep_done"], 1)
                dve.wait_ge(S["prep_done"], done[0])

            v.memset(emb01[0:D, N:NCOL], 0.0)
            v.memset(slots1[:, :, :, NBATCH:SLOTS], 0.0)
            v.memset(cbin[:, ET:EP], 255.0)
            v.memset(pay[:, :, ET:EP], 0.0).then_inc(S["pads_zeroed"], 1)
            dve.wait_ge(S["cols_loaded"], 16)
            chain(v.tensor_scalar(col_bin_f, cols_i[:, :], 1.0 / CB, 0.5 / CB - 0.5, ALU.mult, ALU.add))
            v.tensor_scalar(col_bin_f, col_bin_f, ROUND, ROUND, ALU.add, ALU.subtract)
            dve.wait_ge(S["rows_loaded"], 16)
            chain(v.tensor_scalar(row_bin_f, rows_i[:, :], 1.0 / RB, 0.5 / RB - 0.5, ALU.mult, ALU.add))
            v.tensor_copy(cbin[:, 0:ET], col_bin_f)
            chain(v.tensor_scalar(row_bin_f, row_bin_f, ROUND, ROUND, ALU.add, ALU.subtract))

            def batch(m, k=1):
                return bass.ds(m * BATCH, k * BATCH)

            def along(x, shape, axis):
                return x.unsqueeze(axis).to_broadcast(shape)

            def paired(x):
                return x.rearrange("p (t c) -> p t c", c=2) if len(x.shape) == 2 else x.rearrange("p b (t c) -> p b t c", c=2)

            def bins_of(m, j):
                o = [P, NB1, HB, 2]
                v.tensor_tensor(paired(bins1[:, j]), along(iota_b[:, 0:NB1, :], o, 2), along(paired(cbin[:, batch(m)]), o, 1), ALU.is_equal).then_inc(S["l1_bins"], 1)

            def read_rank(m, j):
                dve.wait_ge(S["l1_rank"], m + 1)
                v.tensor_reduce(rank1[:, batch(m)], ps[:, 4 + j, 0:NB1 * BATCH].rearrange("p (b c) -> p c b", c=BATCH),
                                AX.X, ALU.max).then_inc(S["l1_rank_read"], 1)

            def batch_step(m, j, first=False, last=False):
                if not last:
                    if not (isinstance(m, int) and m == 0):
                        dve.wait_ge(S["l1_spread"], m)
                    bins_of(m + 1, 1 - j)
                read_rank(m, j)
                if not first:
                    dve.wait_ge(S["l1_scattered"], m - 1)
                times_fields(spread1[:, j], bins1[:, j], NB1, pay[:, :, batch(m)], F1).then_inc(S["l1_spread"], 1)
                dve.wait_ge(S["l1_rank_read"], m + 1)
                slot_onehot(j, rank1[:, batch(m)], iota_1[:, :, :]).then_inc(S["l1_slots"], 1)

            def slot_onehot(w, rank, iota):
                o = [P, HB, P, 2]
                return v.tensor_tensor(onehot_slot[:, w], along(iota, o, 1), along(paired(rank), o, 2), ALU.is_equal)

            def times_fields(out, bins, nb, fields, nf):
                o = [P, nb, nf, BATCH]
                return v.tensor_tensor(out.rearrange("p (b f) c -> p b f c", f=nf), along(bins, o, 2), along(fields, o, 1), ALU.mult)

            dve.wait_ge(S["consts_ready"], 1)
            bins_of(0, 0)
            dve.wait_ge(S["vals_loaded"], 16)
            dve.wait_ge(S["value_parts"], 1)
            v.tensor_tensor(rest, vals[:, :], pay[:, 2, 0:ET], ALU.subtract).then_inc(S["value_parts"], 1)
            chain(v.scalar_tensor_tensor(out=row_in_bin, in0=row_bin_f, scalar=-float(RB), in1=rows_i[:, :], op0=ALU.mult, op1=ALU.add))
            v.tensor_scalar(row_in_bin, row_in_bin, float(P), float(PLACE * P), ALU.mult, ALU.add)
            chain(v.scalar_tensor_tensor(out=col_in_bin, in0=col_bin_f, scalar=-float(CB), in1=cols_i[:, :], op0=ALU.mult, op1=ALU.add))
            v.tensor_scalar(pay[:, 0, 0:ET], row_bin_f, 1.0, None, ALU.add)
            v.tensor_tensor(pay[:, 1, 0:ET].bitcast(I16), col_in_bin, row_in_bin, ALU.add)
            dve.wait_ge(S["value_parts"], 3)
            chain(v.tensor_tensor(pay[:, 4, 0:ET], rest, pay[:, 3, 0:ET], ALU.subtract))
            batch_step(0, 0, first=True)
            batch_step(1, 1, first=True)
            with dve.Fori(1, (NBATCH - 1) // 2) as pair:
                m = 2 * pair
                batch_step(m, 0)
                batch_step(m + 1, 1)
            batch_step(NBATCH - 1, 0, last=True)

            dve.wait_ge(S["consts_ready"], 4)
            dve.wait_ge(S["l1_stored"], NBATCH)
            dve.wait_ge(S["l1_scattered"], NBATCH)

            def col_bin(c, f):
                return slots1[:, bass.ds(c, 1), f, :].rearrange("p a c -> p (a c)")

            def bins2_of(c, j):
                v.tensor_tensor(paired(bins2[:, j]), along(iota_b[:, 1:NB2 + 1, :], [P, NB2, SLOTS // 2, 2], 2),
                                along(paired(col_bin(c, 0)), [P, NB2, SLOTS // 2, 2], 1), ALU.is_equal).then_inc(S["l2_bins"], 1)

            def spread_of(c, j, h, first):
                if not first:
                    dve.wait_ge(S["l2_scattered"], c * THIRDS + (h - THIRDS + 1))
                if h == 0:
                    dve.wait_ge(S["l2_bins"], c + 1)
                s = slice(h * BATCH, (h + 1) * BATCH)
                fields = slots1[:, bass.ds(c, 1), 1:F1, s].rearrange("p a f c -> p (a f) c")
                times_fields(spread2[:, h], bins2[:, j, :, s], NB2, fields, F2)

            def rank2_slice(c, h):
                return rank2[:, bass.ds(c, 1), h * BATCH:(h + 1) * BATCH].rearrange("p a c -> p (a c)")

            def ranks2_of(c, j, h, first):
                if first:
                    dve.wait_ge(S["l2_rank"], UNITS * c + 2 * (h + 1))
                    v.tensor_reduce(rk[:, h % 2, :].rearrange("p (k c) -> p k c", k=2),
                                    ps[:, 4:6, 0:NB2 * GW].rearrange("p k (b c) -> p k c b", c=GW), AX.X, ALU.max).then_inc(S["l2_rank_read"], 2)
                    dve.wait_ge(S["l2_rank_read"], UNITS * c + 2 * (h + 1))
                    v.tensor_scalar(rank2_slice(c, h), rk[:, h % 2, :], 2.0 - BIG, None, ALU.add).then_inc(S["rank_rounded"], 1)
                    return
                dve.wait_ge(S["l2_rank_read"], c * UNITS + 2 * (h + 1))
                v.tensor_copy(rank2_slice(c, h), rk[:, (j + h) % 2, :]).then_inc(S["rank_rounded"], 1)

            def slots2_of(c, j, h):
                dve.wait_ge(S["rank_rounded"], c * THIRDS + (h + 1))
                slot_onehot((j + h) % 2, rank2_slice(c, h), iota_s[:, 1:P + 1, :]).then_inc(S["l2_slots"], 1)

            def places_of(k, j):
                dve.wait_ge(S["l2_stored"], k + 1)
                bits = slots2[:, j, 0, :].bitcast(I16)
                v.tensor_scalar(place_c, bits, P - 1, None, ALU.bitwise_and)
                v.tensor_scalar(place_r, bits, 7, None, ALU.logical_shift_right).then_inc(S["l3_places"], 1)

            def onehots3_of(k, j, h, early):
                a, n = SPAN[h]
                u = (j + h) % 2
                if not (early and h < 2):
                    dve.wait_ge(S["l3_built"], k * NG + (4 - NG, 0, 2)[h])
                s, t = slice(a, a + n), slice(0, n // 2)
                if h == 0:
                    dve.wait_ge(S["l3_places"], k + 1)
                if not (early and h == 0):
                    dve.wait_ge(S["l3_ready"], k * THIRDS + h)
                v.tensor_tensor(paired(onehot_r[:, :, 0:n]), along(iota_s[:, PLACE:PLACE + RB, :], [P, RB, n // 2, 2], 2),
                                along(paired(place_r[:, s]), [P, RB, n // 2, 2], 1), ALU.is_equal).then_inc(S["l3_onehot"], 1)
                v.tensor_tensor(onehot_c[:, u, t], along(iota_s[:, 0:P, :], [P, n // 2, P, 2], 1),
                                along(paired(place_c[:, s]), [P, n // 2, P, 2], 2), ALU.is_equal)

            def valued_of(k, j, h):
                a, n = SPAN[h]
                dve.wait_ge(S["l3_onehot"], k * THIRDS + (h + 1))
                o = [P, RB, 3, n]
                v.tensor_tensor(valued[:, (j + h) % 2, :, :, 0:n], along(onehot_r[:, :, 0:n], o, 2),
                                along(slots2[:, j, 1:F2, a:a + n], o, 1), ALU.mult).then_inc(S["l3_ready"], 1)

            def step(c, j, l2=True, l3=True, first=False, early=False, more=True):
                if l2:
                    spread_of(c, j, 0, first)
                    spread_of(c, j, 1, first)
                if l3:
                    places_of(c - 1, 1 - j)
                if l2 and more:
                    bins2_of(c + 1, 1 - j)
                for h in range(THIRDS):
                    if l3:
                        onehots3_of(c - 1, 1 - j, h, early)
                    if l2:
                        ranks2_of(c, j, h, first)
                    if l3:
                        valued_of(c - 1, 1 - j, h)
                    if l2:
                        slots2_of(c, j, h)
                        if h == 0:
                            spread_of(c, j, 2, first)

            bins2_of(0, 0)
            step(0, 0, l3=False, first=True)
            step(1, 1, early=True)
            with dve.Fori(1, (NB1 - 2) // 2) as pair:
                c = 2 * pair
                step(c, 0)
                step(c + 1, 1)
            step(NB1 - 2, 0)
            step(NB1 - 1, 1, more=False)

            parts = S["flag_parts"]
            v.tensor_reduce(worst[:, 2:3], cols_i[:, :], AX.X, ALU.max)
            v.tensor_reduce(worst[:, 3:4], rows_i[:, :], AX.X, ALU.max)
            v.tensor_reduce(worst[:, 0:1], rank1[:, :], AX.X, ALU.max)
            v.tensor_reduce(worst[:, 1:2], rank2[:, :, :], AX.XY, ALU.max).then_inc(parts, 1)
            dve.wait_ge(parts, 1)
            v.tensor_scalar(worst[:, 0:1], worst[:, 0:1], 2.0 - BIG, None, ALU.add).then_inc(parts, 1)
            dve.wait_ge(parts, 2)
            v.tensor_tensor(over[:, 0:1], worst[:, 0:1], worst[:, 1:2], ALU.max)
            v.tensor_tensor(over[:, 1:2], worst[:, 2:3], worst[:, 3:4], ALU.max).then_inc(parts, 1)
            dve.wait_ge(parts, 3)
            v.tensor_scalar(over[:, 0:1], over[:, 0:1], P + 0.5, None, ALU.is_gt)
            v.tensor_scalar(over[:, 1:2], over[:, 1:2], GRAPH - 0.5, None, ALU.is_gt).then_inc(parts, 1)
            dve.wait_ge(parts, 4)
            v.tensor_tensor(over[:, 2:3], over[:, 0:1], over[:, 1:2], ALU.add).then_inc(S["flag_vec"], 1)
            step(NB1, 0, l2=False)
            dve.wait_ge(S["flag_sum"], 1)
            v.tensor_copy(flag[:, :], ps[0:1, 4, 0:1]).then_inc(S["flag_ready"], 1)
            dve.wait_ge(S["flag_ready"], 1)
            overflow = dve.value_load(flag[0:1, 0:1])

            def fallback(l):
                def stage(t):
                    v.tensor_copy(s_col[:, :], cols_i[:, bass.ds(t, 1)])
                    v.tensor_copy(s_rv[:, 0:1], rows_i[:, bass.ds(t, 1)])
                    v.tensor_copy(s_rv[:, 1:2], vals[:, bass.ds(t, 1)]).then_inc(S["s_staged"], 1)

                def products(t, first):
                    n = t + (l * ET + 1)
                    dve.wait_ge(S["s_staged"], n)
                    dve.wait_ge(S["s_gathered"], n * 16)
                    v.tensor_scalar(s_gv[:, :], s_g[:, :], s_rv[:, 1:2], None, ALU.mult).then_inc(S["s_scaled"], 1)
                    for b in range(OB):
                        if not (first and b < 2):
                            dve.wait_ge(S["s_summed"], t * OB + (l * ET * OB + b - 1))
                        v.tensor_scalar(lk[:, b % 2, :], s_iota, s_rv[:, 0:1], -float(b * BANK), ALU.subtract, ALU.is_equal).then_inc(S["s_onehot"], 1)
                    dve.wait_ge(S["s_summed"], t * OB + (l * ET * OB + OB))

                dve.wait_ge(S["s_counted"], l + 1)
                stage(0)
                products(0, l == 0)
                with dve.Fori(1, ET) as t:
                    stage(t)
                    products(t, False)
                v.tensor_copy(stack[0:D, 0:N], ps[0:D, :, :].rearrange("p b c -> p (b c)")[:, 0:N]).then_inc(S["s_side"], 1)
                dve.wait_ge(S["s_side"], l + 1)

            for l in range(L):
                if l == 0:
                    dve.wait_ge(S["l2_scattered"], NB1 * THIRDS)
                    dve.wait_ge(S["l2_slots"], NB1 * THIRDS)
                    v.memset(stack[0:D, GRAPH:NCOL], 0.0)
                dve.wait_ge(S["side_added"], NB1 * (l + 1))
                if l:
                    dve.wait_ge(S["e_copied"], NCH)
                for q in range(0, SQ, 2):
                    v.tensor_copy(stack[0:D, q * CHUNK:(q + 1) * CHUNK], side_piece(q)).then_inc(S["side_ready"], 1)
                dve.wait_ge(S["side_ready"], (l + 1) * SQ)
                with dve.If(overflow):
                    fallback(l)
                ego = emb01 if l == 0 else emb2
                if l:
                    dve.wait_ge(S["emb1_copied"], 1)

                def mult(k):
                    a, w = CH[k]
                    v.tensor_tensor(stack[D:P, a:a + w], ego[0:D, a:a + w], stack[0:D, a:a + w], ALU.mult).then_inc(S["stack_ready"], 1)

                def leaky(k):
                    n = l * NCH + k
                    w = CH[k][1]
                    dve.wait_ge(S["zb_ready"], n + 1)
                    if k >= 2:
                        dve.wait_ge(S["e_ready" if l else "nm2_ready"], n - 1)
                    v.scalar_tensor_tensor(out=lk[:, k % 2, 0:w], in0=zb[:, k % 2, 0:w], scalar=0.01, in1=zb[:, k % 2, 0:w],
                                           op0=ALU.mult, op1=ALU.max).then_inc(S["lk_ready"], 1)

                def to_node_order(k):
                    a, w = CH[k]
                    dve.wait_ge(S["nm2_ready"], k + 1)
                    v.tensor_copy(ego_nm[0:CB, a // CB:(a + w) // CB, :],
                                  ps[0:CB, node_bank(k), 0:w // CB * D].rearrange("p (t d) -> p t d", d=D)).then_inc(S["nm2_copied"], 1)

                mult(0)
                mult(1)
                for k in range(NCH):
                    leaky(k)
                    if k + 2 < NCH:
                        mult(k + 2)
                    if l == 0 and k:
                        to_node_order(k - 1)
                if l == 0:
                    to_node_order(NCH - 1)

            def bank_half(ut, h):
                return ps[:, ut % 2 * Q + h * HQ:ut % 2 * Q + (h + 1) * HQ, 0:QC]

            for ut in range(UT):
                dve.wait_ge(S["score_ready"], 2 * ut + 1)
                v.tensor_reduce(sc[:, ut, 0:1], bank_half(ut, 0), AX.XY, ALU.max).then_inc(S["max_parts"], 1)
                dve.wait_ge(S["max_parts"], 3 * ut + 1)
                v.tensor_scalar(sc[:, ut, 2:3], sc[:, ut, 0:1], -1.0, None, ALU.mult).then_inc(S["max_parts"], 1)
                dve.wait_ge(S["score_ready"], 2 * ut + 2)
                v.tensor_reduce(sc[:, ut, 1:2], bank_half(ut, 1), AX.XY, ALU.max).then_inc(S["max_parts"], 1)
                dve.wait_ge(S["max_parts"], 3 * ut + 3)
                v.scalar_tensor_tensor(out=sc[:, ut, 3:4], in0=sc[:, ut, 1:2], scalar=-1.0, in1=sc[:, ut, 2:3],
                                       op0=ALU.mult, op1=ALU.min).then_inc(S["max_ready"], 1)
                dve.wait_ge(S["shift_ready"], ut + 1)
                if ut >= 2:
                    dve.wait_ge(stored_out[ut % 2], 32 * (ut // 2))
                v.tensor_scalar(res[:, ut % 2, 0:HQ * QC].rearrange("p (q c) -> p q c", q=HQ), bank_half(ut, 0),
                                sc[:, ut, 6:7], None, ALU.add).then_inc(S["left_ready"], 1)

        @block.scalar
        def _(act):
            def copy(o, i):
                return nc.scalar.activation(o, i, ACT.Copy)

            nc.scalar.preload_act_table_set("natural_log_exp_and_others")

            act.wait_ge(S["vals_loaded"], 16)
            copy(pay[:, 2, 0:ET], vals[:, :]).then_inc(S["value_parts"], 1)
            act.wait_ge(S["value_parts"], 2)
            copy(pay[:, 3, 0:ET], rest).then_inc(S["value_parts"], 1)
            act.wait_ge(S["pads_zeroed"], 1)

            def read_count1(m, j, first=False):
                act.wait_ge(S["l1_counted"], m + 1)
                if not first:
                    act.wait_ge(S["l1_rank"], m - 1)
                copy(tile_count1[0:BATCH, j, :], ps[0:BATCH, j, 0:NB1]).then_inc(S["l1_count_read"], 1)

            def store1(m, j):
                act.wait_ge(S["l1_scattered"], m + 1)
                copy(slots1[:, :, :, bass.ds(m, 1)].rearrange("p b f a -> p (b f a)"), ps[:, 6 + j, 0:NB1 * F1]).then_inc(S["l1_stored"], 1)

            read_count1(0, 0, True)
            read_count1(1, 1, True)
            read_count1(2, 0)
            store1(0, 0)
            def piece(i):
                o = 2 + i % 2
                if i < NTG:
                    act.wait_ge(S["tr_ready"], i + 1)
                    w = min(TG * P, N - i * TG * P)
                    copy(emb01[0:D, i * TG * P:i * TG * P + w], ps[0:D, o, 0:w]).then_inc(S["tr_copied"], 1)
                elif i < NTG + L:
                    act.wait_ge(S["tr_ready"], i + 1)
                    copy(wT[:, i - NTG, :], ps[:, o, 0:P]).then_inc(S["tr_copied"], 1)
                else:
                    g = i - NTG - L
                    act.wait_ge(S["nm_ready"], g + 1)
                    n = min(GW, NT - g * GW)
                    copy(ego_nm[0:CB, g * GW:g * GW + n, :],
                         ps[0:CB, o, 0:n * D].rearrange("p (t d) -> p t d", d=D)).then_inc(S["nm_copied"], 1)

            at_pair = 1
            for n, stop in enumerate(STOPS + [(NBATCH - 1) // 2]):
                with act.Fori(at_pair, stop) as pair:
                    m = 2 * pair
                    read_count1(m + 1, 1)
                    store1(m - 1, 1)
                    read_count1(m + 2, 0)
                    store1(m, 0)
                at_pair = stop
                for i in range(2 * n, min(2 * n + 2, NPIECE)):
                    piece(i)
            store1(NBATCH - 2, 1)
            store1(NBATCH - 1, 0)

            def store3(k, j, g, early):
                a, n = GROUPS[g]
                act.wait_ge(S["l3_built"], k * NG + (g + 1))
                if g == 0 and not early:
                    act.wait_ge(S["side_added"], k - 1)
                    act.wait_ge(block_saved[j], (k - j) * 8)
                copy(work[:, j, a * RB:(a + n) * RB], ps[:, 6 + group_bank(g), 0:n * RB]).then_inc(S["l3_stored"], 1)

            def store2(c, j, early):
                act.wait_ge(S["l2_scattered"], c * THIRDS + THIRDS)
                if not early:
                    act.wait_ge(S["l3_ready"], (c - 1) * THIRDS)
                copy(slots2[:, j], ps[:, 3, 0:NB2 * F2].rearrange("p (b f) -> p f b", f=F2)).then_inc(S["l2_stored"], 1)

            def read_ranks(c, j, u):
                h = u // 2
                w = (j + h) % 2
                act.wait_ge(S["l2_rank"], c * UNITS + (u + 1))
                if u % 2 == 0:
                    act.wait_ge(S["rank_rounded"], c * THIRDS + (h - 1))
                    act.wait_ge(S["l2_rank_read"], c * UNITS + (u - 2))
                for i in range(GW):
                    t = u % 2 * GW + i
                    x = nc.scalar.activation(matched[:, w, t, :], ps[:, 4 + u % 2, 0:NB2 * GW].rearrange("p (b c) -> p b c", c=GW)[:, :, i],
                                             ACT.Relu, bias=below[:, :], accum_out=rk[:, w, t:t + 1])
                x.then_inc(S["l2_rank_read"], 1)

            def read_counts(c):
                act.wait_ge(S["l2_counted"], c + 1)
                copy(tile_count[0:SLOTS, :], ps[0:SLOTS, 6, 0:NB2]).then_inc(S["l2_count_read"], 1)

            def step(c, j, l2=True, l3=True, early3=False, early2=False, first=False, more=True):
                def ranks(u):
                    if l2 and not first:
                        read_ranks(c, j, u)

                def groups(*which):
                    for g in which if l3 else ():
                        store3(c - 1, 1 - j, g, early3)

                ranks(2)
                ranks(3)
                groups(0, 1)
                ranks(4)
                ranks(5)
                groups(2, 3)
                if l2 and more:
                    read_counts(c + 1)
                groups(4)
                if l2 and more:
                    read_ranks(c + 1, 1 - j, 0)
                if l2:
                    store2(c, j, early2)
                groups(5, 6)
                if l2 and more:
                    read_ranks(c + 1, 1 - j, 1)

            act.wait_ge(S["consts_ready"], 4)
            read_counts(0)
            step(0, 0, l3=False, early2=True, first=True)
            step(1, 1, early3=True, early2=True)
            step(2, 0, early3=True)
            step(3, 1)
            with act.Fori(2, (NB1 - 2) // 2) as pair:
                c = 2 * pair
                step(c, 0)
                step(c + 1, 1)
            step(NB1 - 2, 0)
            step(NB1 - 1, 1, more=False)
            step(NB1, 0, l2=False)

            for l in range(L):
                act.wait_ge(S["side_added"], NB1 * (l + 1))
                if l:
                    act.wait_ge(S["z_ready"], l * NCH)
                for q in range(1, SQ, 2):
                    copy(stack[0:D, q * CHUNK:(q + 1) * CHUNK], side_piece(q)).then_inc(S["side_ready"], 1)

                def add_bias(k):
                    n = l * NCH + k
                    w = CH[k][1]
                    act.wait_ge(S["z_ready"], n + 1)
                    if n >= 2:
                        act.wait_ge(S["lk_ready"], n - 1)
                    nc.scalar.activation(zb[:, k % 2, 0:w], ps[:, 4 + k % 2, 0:w], ACT.Identity, bias=bias[:, l:l + 1]).then_inc(S["zb_ready"], 1)

                add_bias(0)
                add_bias(1)
                for k, (a, w) in enumerate(CH):
                    act.wait_ge(S["e_ready"], l * NCH + k + 1)
                    new = emb2[0:D, a:a + w] if l else emb01[D:P, a:a + w]
                    hw = (w + 1) // 2
                    copy(new[:, 0:hw], ps[0:D, 6 + k % 2, 0:hw])
                    copy(new[:, hw:w], ps[D:P, 6 + k % 2, 0:w - hw]).then_inc(S["e_copied"], 1)
                    if k + 2 < NCH:
                        add_bias(k + 2)
                if l == 0:
                    act.wait_ge(S["e_copied"], NCH)
                    copy(emb2[0:D, :], emb01[D:P, :]).then_inc(S["emb1_copied"], 1)

            act.wait_ge(S["z_ready"], L * NCH)
            for ut in range(UT):
                act.wait_ge(S["max_ready"], ut + 1)
                if ut:
                    act.wait_ge(S["exp_ready"], ut)
                nc.scalar.activation(junk.rearrange("p (q c) -> p q c", q=Q), ps[:, ut % 2 * Q:ut % 2 * Q + Q, 0:QC], ACT.Exp,
                                     bias=sc[:, ut, 3:4], accum_out=sc[:, ut, 4:5]).then_inc(S["exp_ready"], 1)
                act.wait_ge(S["exp_ready"], ut + 1)
                nc.scalar.activation(sc[:, ut, 5:6], sc[:, ut, 4:5], ACT.Ln).then_inc(S["ln_ready"], 1)
                act.wait_ge(S["ln_ready"], ut + 1)
                nc.scalar.activation(sc[:, ut, 6:7], sc[:, ut, 5:6], ACT.Identity, bias=sc[:, ut, 3:4], scale=-1.0).then_inc(S["shift_ready"], 1)
                act.wait_ge(S["shift_ready"], ut + 1)
                if ut >= 2:
                    act.wait_ge(stored_out[ut % 2], 32 * (ut // 2))
                nc.scalar.activation(res[:, ut % 2, HQ * QC:NI].rearrange("p (q c) -> p q c", q=HQ),
                                     ps[:, ut % 2 * Q + HQ:ut % 2 * Q + Q, 0:QC], ACT.Identity, bias=sc[:, ut, 6:7]).then_inc(S["right_ready"], 1)


_INS = ["r_user_indices", "L0_rec_item_indices", "L0_rec_adj_rows", "L0_rec_adj_cols", "L0_rec_adj_vals",
        "L0_rec_user_emb", "L0_rec_item_emb", "L0_rec_gc_W", "L0_rec_gc_b", "L0_rec_bi_W", "L0_rec_bi_b"]


def kernel(**inputs):
    import numpy as np
    import concourse.bacc as bacc
    from concourse.bass_utils import run_bass_kernel_spmd

    nc = bacc.Bacc("TRN2", target_bir_lowering=False, num_devices=1)
    arrays, args = {}, []
    for name in _INS:
        a = np.ascontiguousarray(inputs[name])
        arrays[f"in_{name}"] = a
        args.append(nc.dram_tensor(f"in_{name}", a.shape, mybir.dt.from_np(a.dtype), kind="ExternalInput").ap())
    shape = (inputs["r_user_indices"].shape[0], inputs["L0_rec_item_indices"].shape[0])
    args.append(nc.dram_tensor("out_scores", shape, F32, kind="ExternalOutput").ap())
    build(nc, *args)
    r = run_bass_kernel_spmd(nc, [arrays], core_ids=[0])
    return r.results[0]["out_scores"]
```
